# Optimizing a Trainium2 kernel written in Bass

```python
import numpy as np
import jax
import jax.numpy as jnp

def _softmax(x, axis=-1):
    return jax.nn.softmax(x, axis=axis)

def _gelu(x):
    return jax.nn.gelu(x, approximate=True)

def _silu(x):
    return jax.nn.silu(x)

def _sigmoid(x):
    return jax.nn.sigmoid(x)

def _layernorm(x, axis=-1, eps=1e-05):
    m = jnp.mean(x, axis=axis, keepdims=True)
    v = jnp.var(x, axis=axis, keepdims=True)
    return (x - m) / jnp.sqrt(v + eps)

def _scatter_add(tgt, idx, src, axis=0):
    return tgt.at[idx].add(src)

def _segment_sum(src, seg, n):
    return jax.ops.segment_sum(src, seg, n)
kernel_name = 'mk_adj_preln_d4_adj_r2_b6beeb'

def setup_inputs(seed: int=0):
    np.random.seed(seed)
    _w = jnp.asarray

    def _rec_inputs():
        import jax
        import jax.numpy as jnp
        _gk = jax.random.key(seed)
        x = -9.806e-05 + 1 * jax.random.normal(jax.random.fold_in(_gk, 1), (128, 128, 64), jnp.float32)
        _a = jax.random.bernoulli(jax.random.fold_in(_gk, 2), 0.125, (128, 128, 128))
        _a = jnp.logical_or(_a, jnp.swapaxes(_a, -1, -2))
        _a = jnp.logical_or(_a, jnp.eye(128, dtype=bool))
        _af = _a.astype(jnp.float32)
        _af = _af * jax.random.uniform(jax.random.fold_in(_gk, 3), (128, 128, 128), jnp.float32, 0.05, 0.158154)
        adj = _af
        return (x, adj)
    x, adj = _rec_inputs()

    def _L0_gnn_setup():
        import jax, jax.numpy as jnp
        import numpy as np
        B, N, C_IN, C_OUT, K = (8, 512, 64, 64, 4)
        key = jax.random.key(seed)
        k1, k2, k3 = jax.random.split(key, 3)
        x = jax.random.normal(k1, (B, N, C_IN), dtype=jnp.float32)
        L = jax.random.normal(k2, (B, N, N), dtype=jnp.float32) * (1.0 / np.sqrt(N))
        theta = jax.random.normal(k3, (K, C_IN, C_OUT), dtype=jnp.float32) * np.sqrt(2.0 / C_IN)
        return {'x': x, 'L': L, 'theta': theta}
    _L0_gnn_all = _L0_gnn_setup()
    _L0_gnn_in = {k: v for k, v in _L0_gnn_all.items() if k in ('theta',)}
    del _L0_gnn_all

    def _L1_gnn_setup():
        import jax, jax.numpy as jnp
        import numpy as np
        B, N, F, U = (16, 1024, 64, 64)
        key = jax.random.key(seed)
        k1, k2, k3 = jax.random.split(key, 3)
        node_features = jax.random.normal(k1, (B, N, F), dtype=jnp.float32)
        adjacency_matrix = (jax.random.uniform(k2, (B, N, N)) < 0.01).astype(jnp.float32)
        kernel = jax.random.normal(k3, (F, U), dtype=jnp.float32) * (1.0 / np.sqrt(F))
        return {'node_features': node_features, 'adjacency_matrix': adjacency_matrix, 'kernel': kernel}
    _L1_gnn_all = _L1_gnn_setup()
    _L1_gnn_in = {k: v for k, v in _L1_gnn_all.items() if k in ('kernel',)}
    del _L1_gnn_all

    def _L2_gnn_setup():
        import jax, jax.numpy as jnp
        import numpy as np
        NEG_INF = -1000000000.0
        EPS = 1e-07
        ADJ_SCALE = 10.0
        key = jax.random.key(seed)
        k1, k2, k3 = jax.random.split(key, 3)
        B, N, D = (4, 2048, 64)
        x = jax.random.normal(k1, (B, N, D), dtype=jnp.float32)
        adj = (jax.random.uniform(k2, (B, N, N)) < 64.0 / N).astype(jnp.float32)
        beta = jax.random.uniform(k3, (1,), dtype=jnp.float32)
        return {'x': x, 'adj': adj, 'beta': beta}
    _L2_gnn_all = _L2_gnn_setup()
    _L2_gnn_in = {k: v for k, v in _L2_gnn_all.items() if k in ('beta',)}
    del _L2_gnn_all

    def _L3_gnn_setup():
        import jax, jax.numpy as jnp
        import numpy as np
        N_RBF = 150
        GAMMA = 10.0
        LOG2 = float(np.log(2.0))

        def ssp(v):
            return jax.nn.softplus(v) - LOG2
        key = jax.random.key(seed)
        k1, k2, k3, k4 = jax.random.split(key, 4)
        B, N, F = (16, 128, 64)
        x = jax.random.normal(k1, (B, N, F), dtype=jnp.float32)
        distances = jax.random.uniform(k2, (B, N, N), dtype=jnp.float32)
        W1 = jax.random.normal(k3, (N_RBF, 64), dtype=jnp.float32) / np.sqrt(N_RBF)
        b1 = jnp.zeros((64,), dtype=jnp.float32)
        W2 = jax.random.normal(k4, (64, 64), dtype=jnp.float32) / np.sqrt(64)
        b2 = jnp.zeros((64,), dtype=jnp.float32)
        return {'x': x, 'distances': distances, 'W1': W1, 'b1': b1, 'W2': W2, 'b2': b2}
    _L3_gnn_all = _L3_gnn_setup()
    _L3_gnn_in = {k: v for k, v in _L3_gnn_all.items() if k in ('W1', 'b1', 'W2', 'b2')}
    del _L3_gnn_all
    return {'x': x, 'adj': adj, 'L0_gnn_theta': _L0_gnn_in['theta'], 'L1_gnn_kernel': _L1_gnn_in['kernel'], 'L2_gnn_beta': _L2_gnn_in['beta'], 'L3_gnn_W1': _L3_gnn_in['W1'], 'L3_gnn_b1': _L3_gnn_in['b1'], 'L3_gnn_W2': _L3_gnn_in['W2'], 'L3_gnn_b2': _L3_gnn_in['b2']}

def reference(x, adj, L0_gnn_theta, L1_gnn_kernel, L2_gnn_beta, L3_gnn_W1, L3_gnn_b1, L3_gnn_W2, L3_gnn_b2):
    import jax
    import jax.numpy as jnp

    def _L0_gnn_ref(x, L, theta):
        import jax, jax.numpy as jnp
        import numpy as np
        B, N, C_IN, C_OUT, K = (8, 512, 64, 64, 4)
        k_orders = theta.shape[0]
        z_prev = x
        out = jnp.matmul(z_prev, theta[0])
        if k_orders > 1:
            z_curr = jnp.matmul(L, x)
            out = out + jnp.matmul(z_curr, theta[1])
            for k in range(2, k_orders):
                z_next = 2.0 * jnp.matmul(L, z_curr) - z_prev
                out = out + jnp.matmul(z_next, theta[k])
                z_prev, z_curr = (z_curr, z_next)
        return out

    def _L1_gnn_ref(node_features, adjacency_matrix, kernel):
        import jax, jax.numpy as jnp
        import numpy as np
        B, N, F, U = (16, 1024, 64, 64)
        n = adjacency_matrix.shape[-1]
        adj = adjacency_matrix + jnp.eye(n, dtype=adjacency_matrix.dtype)
        row_sum = jnp.sum(adj, axis=-1)
        d_inv_sqrt = jnp.where(row_sum > 0, row_sum ** (-0.5), 0.0)
        norm_adj = d_inv_sqrt[:, :, None] * adj * d_inv_sqrt[:, None, :]
        transformed = jnp.einsum('bnf,fu->bnu', node_features, kernel)
        out = jnp.einsum('bnm,bmu->bnu', norm_adj, transformed)
        return jax.nn.relu(out)

    def _L2_gnn_ref(x, adj, beta):
        import jax, jax.numpy as jnp
        import numpy as np
        NEG_INF = -1000000000.0
        EPS = 1e-07
        ADJ_SCALE = 10.0
        norm2 = jnp.linalg.norm(x, axis=-1, keepdims=True)
        dots = jnp.einsum('bnd,bmd->bnm', x, x)
        cos = dots / (norm2 * jnp.swapaxes(norm2, -1, -2) + EPS)
        mask = jnp.where(cos < 0, NEG_INF, 0.0)
        masked = beta[0] * cos + mask + ADJ_SCALE * adj
        P = jax.nn.softmax(masked, axis=2)
        return jnp.einsum('bnm,bmd->bnd', P, x)

    def _L3_gnn_ref(x, distances, W1, b1, W2, b2):
        import jax, jax.numpy as jnp
        import numpy as np
        N_RBF = 150
        GAMMA = 10.0
        LOG2 = float(np.log(2.0))

        def ssp(v):
            return jax.nn.softplus(v) - LOG2
        centers = 0.1 * jnp.arange(N_RBF, dtype=distances.dtype)
        e_k = jnp.exp(-GAMMA * (distances[..., None] - centers) ** 2)
        h = ssp(jnp.einsum('bijk,kf->bijf', e_k, W1) + b1)
        w_l = ssp(jnp.einsum('bijf,fg->bijg', h, W2) + b2)
        return jnp.sum(x[:, :, None, :] * w_l, axis=2)
    h = jnp.maximum(_layernorm(x, axis=-1), 0.0)
    x = x + _L0_gnn_ref(h, adj, L0_gnn_theta)
    h = jnp.maximum(_layernorm(x, axis=-1), 0.0)
    x = x + _L1_gnn_ref(h, adj, L1_gnn_kernel)
    h = jnp.maximum(_layernorm(x, axis=-1), 0.0)
    x = x + _L2_gnn_ref(h, adj, L2_gnn_beta)
    h = jnp.maximum(_layernorm(x, axis=-1), 0.0)
    x = x + _L3_gnn_ref(h, adj, L3_gnn_W1, L3_gnn_b1, L3_gnn_W2, L3_gnn_b2)
    return x

_drawn_inputs = setup_inputs


def setup_inputs(seed=0):
    import zlib

    import numpy as np

    out = dict(_drawn_inputs(seed))
    spreads = {'L3_gnn_b1': (0.0, 0.316), 'L3_gnn_b2': (0.0, 0.1)}
    factors = {'L1_gnn_kernel': 8.0}
    for name, (base, spread) in spreads.items():
        noise = np.random.default_rng([zlib.crc32(name.encode()), seed]).standard_normal(out[name].shape)
        drawn = base * np.exp(spread * noise) if base else spread * noise
        out[name] = jnp.asarray(drawn.astype(out[name].dtype))
    for name, factor in factors.items():
        out[name] = (out[name] * factor).astype(out[name].dtype)
    return out
```

```python
import concourse.bass as bass
from concourse import mybir
from contextlib import ExitStack

F32 = mybir.dt.float32
F16 = mybir.dt.float16
I32 = mybir.dt.int32
ALU = mybir.AluOpType
ACT = mybir.ActivationFunctionType
AX = mybir.AxisListType

N = 128
F = 64
G = 4
KF = 32
KALL = 150
DMAX = 0.2
GAMMA = 10.0
LOG2 = 0.6931471805599453
EPS_LN = 1e-5
EPS_COS = 1e-7
TOP = 56
BLOCKS = [(0, 28, 128), (28, 4, 112), (32, 4, 80), (36, 4, 32), (40, 4, 16), (44, 4, 8), (48, 8, 4)]
COLS = sum(s * r for _, s, r in BLOCKS)
UNITS = COLS // 512
QH = COLS // 4
LQ_PARTS = 3
QP = QH // LQ_PARTS
NPART = 4
PW = NPART * TOP
DSCALE = 256.0
QSCALE = 1024.0
C_ID, C_MISS, C_NMASK, C_BIAS, C_EMAX, C_CAP, C_NLOG, C_CEN = 0, 128, 256, 768, 769, 770, 771, 772
NC32 = 774
H_ID, H_P128, H_N128, H_CMAT, H_IOTA, H_ARGW = 0, 128, 256, 384, 512, 640
NC16 = 768

PE_AT = {"adjT": 0, "delta": 3, "hT0": 3, "rank_parts0": 5, "cheb3": 7, "rank_parts1": 7, "cheb2": 7, "cheb1": 9,
    "h2T_mm": 9, "nT_mm": 13, "cheb0": 15, "row_sums": 17, "sT_mm": 17, "D_mm": 17, "sperm": 19, "dots": 19,
    "permT": 22, "hT1": 25, "pT_mm": 26, "hw": 28, "att_mm": 28, "gcn_mm": 31}
ACT_AT = {"copy_adjT": 3, "negatives": 5, "log22": 6, "copy_hT0": 7, "copy_ranked0": 7, "twice_b3": 8,
    "copy_ranked1": 9, "twice_b2": 9, "copy_h2T": 12, "copy_nT": 17, "copy_sR": 20, "log_D": 20, "recip_D": 21,
    "log20": 22, "copy_permT": 25, "copy_hT1": 27, "exp_logits": 27, "copy_pT": 28, "log21": 29}
DVE_AT = {"counts": 0, "lnA1": 0, "split_parts": 1, "lnB1": 1, "ln_var_A1": 2, "ln_out_A1": 3, "check_sorted": 5,
    "ranks": 5, "perms": 5, "ln_var_B1": 5, "ln_out_B1": 6, "sum_slots": 7, "check_ranked": 8, "cheb_d1": 10,
    "norms": 10, "max0": 13, "remove0": 14, "max1": 16, "cheb_x1": 17, "norm_rows": 17, "remove1": 17, "degrees": 18,
    "ln_var_A2": 19, "max2": 19, "degree_inv": 20, "combine": 20, "cosines": 20, "remove2": 20, "ln_out_A2": 22,
    "logits": 22, "row_max": 22, "max3": 22, "shift": 23, "remove3": 23, "max4": 24, "remove4": 25, "max5": 27,
    "gcn_y": 28, "remove5": 28, "attend": 30, "max6": 30, "ln_var_B2": 31, "gcn_x2": 34, "ln_out_B2": 35}


def tables():
    import numpy as np
    c = np.zeros((128, NC32), np.float32)
    h = np.zeros((128, NC16), np.float16)
    slots = np.zeros(128)
    for _, s, r in BLOCKS:
        slots[:r] += s
    c[:, C_ID:C_ID + 128] = np.eye(128)
    c[:, C_MISS:C_MISS + 128] = N - slots[None, :]
    for g in range(G):
        c[g, C_NMASK + 128 * g:C_NMASK + 128 * g + 128] = 1.0
    k = np.arange(128) % KF
    cen = (np.float32(0.1) * np.arange(KALL, dtype=np.float32)).astype(np.float64)
    c[:, C_BIAS] = -GAMMA * cen[k] ** 2
    c[:, C_EMAX] = np.exp(-GAMMA * np.maximum(cen[k] - DMAX, 0) ** 2) * 1.0001
    c[:, C_CAP] = slots
    c[:, C_NLOG] = -LOG2
    c[:, C_CEN] = -cen[:128]
    c[:KALL - 128, C_CEN + 1] = -cen[128:]
    i = np.arange(128)
    h[:, H_ID:H_ID + 128] = np.eye(128)
    h[:, H_P128:H_P128 + 128] = 128.0
    h[:, H_N128:H_N128 + 128] = -128.0
    h[:, H_CMAT:H_CMAT + 128] = i[:, None] - i[None, :]
    h[:, H_IOTA:H_IOTA + 128] = i[None, :]
    for g in range(G):
        for q, w in enumerate((2 * GAMMA * 0.1 / DSCALE, 2 * GAMMA * 0.1 / DSCALE, -GAMMA / QSCALE, -GAMMA / QSCALE)):
            h[NPART * g + q, H_ARGW + KF * g:H_ARGW + KF * (g + 1)] = w * (np.arange(KF) if q < 2 else 1.0)
    return c, h


def adjacency_layers(nc, x, adj, theta, wk, beta, w1, b1, w2, b2, c32, c16, out):
    B = x.shape[0]
    NT = B // G
    assert B % (2 * G) == 0 and NT >= 8 and UNITS == 9
    rows_dram = [nc.dram_tensor(f"arg_rows{p}", [NPART * G, COLS], F16, kind="Internal").ap() for p in range(2)]
    s_dram = nc.dram_tensor("s_rows", [B * 8, 4, 4, F], F32, kind="Internal").ap()
    scratch = nc.dram_tensor("x3_h4", [NT, 128, 2, G * F], F32, kind="Internal").ap()

    with ExitStack() as ctx:
        def sb(name, shape, dt=F32):
            return ctx.enter_context(nc.sbuf_tensor(name, shape, dt))

        def sem(name):
            return ctx.enter_context(nc.semaphore(name))

        c32s = sb("c32s", [128, NC32])
        c16s = sb("c16s", [128, NC16], F16)
        w1z = sb("w1z", [128, 2, 128])
        w2bd = sb("w2bd", [128, 128])
        b1c = sb("b1c", [128, 1])
        b2c = sb("b2c", [128, 1])
        b2p = sb("b2p", [128, 1])
        thin = sb("thin", [128, 4, F])
        th = sb("th", [128, 4, 128])
        wks = sb("wks", [128, 128])
        betac = sb("betac", [128, 1])
        onesc = sb("onesc", [128, 1])
        kmat = sb("kmat", [128, 2, 128])
        setup = sb("setup", [128, 16])
        wpos1, wneg1, wpos2, wneg2 = (sb(n, [128, 128]) for n in ("wpos1", "wneg1", "wpos2", "wneg2"))
        epsc = sb("epsc", [128, 1])
        bad = sb("bad", [128, 1])
        badneg = sb("badneg", [128, 1])
        flagf = sb("flagf", [1, 1])
        flagi = sb("flagi", [1, 1], I32)

        adj_t = [sb(f"adj_t{p}", [128, G, N]) for p in range(2)]
        x_t = [sb(f"x_t{p}", [128, G, F]) for p in range(2)]
        srt_w = sb("srt_w", [128, G, N])
        gate = sb("gate", [128, 1])
        srt = sb("srt", [128, G, TOP])
        nz = sb("nz", [128, G, TOP])
        cnt = sb("cnt", [128, G])
        srt_c = sb("srt_c", [128, G, TOP])
        dsq = sb("dsq", [128, G, TOP])
        parts = sb("parts", [128, G * PW + G], F16)
        diag = sb("diag", [128, G, 128], F16)
        rank = sb("rank", [128, G])
        junk = sb("junk", [128, G, 128], F16)
        junk4 = sb("junk4", [128, 4])
        junka = sb("junka", [128, G * N])
        perm = sb("perm", [128, G, 128], F16)
        perm_t = [sb(f"perm_t{p}", [128, G, 128]) for p in range(2)]
        parts_r = sb("parts_r", [128, G * PW + G], F16)
        argin = [sb(f"argin{p}", [128, COLS], F16) for p in range(2)]

        adj_tr = sb("adj_tr", [128, G, N])
        adj10 = [sb(f"adj10_{p}", [128, G, N]) for p in range(2)]
        ln_sum = sb("ln_sum", [128, G])
        xc = sb("xc", [128, G, F])
        sq = sb("sq", [128, G, F])
        var = sb("var", [128, G])
        rstd = sb("rstd", [128, G])
        expo = sb("expo", [128, G])
        ten = sb("ten", [128, 1])
        half = sb("half", [128, G])
        ln2_sum = sb("ln2_sum", [128, G])
        xc2 = sb("xc2", [128, G, F])
        sq2 = sb("sq2", [128, G, F])
        var2 = sb("var2", [128, G])
        rstd2 = sb("rstd2", [128, G])
        hcur = sb("hcur", [128, G, F])
        hT = sb("hT", [128, 2, 128])
        b3x2 = sb("b3x2", [128, G, F])
        b2x2 = sb("b2x2", [128, G, F])
        d1 = sb("d1", [128, G, F])
        x1 = sb("x1", [128, G, F])
        rsp = sb("rsp", [128, G])
        rsm = sb("rsm", [128, G])
        dinv0 = sb("dinv0", [128, G])
        dinv = sb("dinv", [128, G])
        ysc = sb("ysc", [128, G, F])
        gcn = sb("gcn", [128, G, F])
        x2 = [sb(f"x2_{p}", [128, G, F]) for p in range(2)]
        h2 = sb("h2", [128, G, F])
        h2T = sb("h2T", [128, G, 128])
        n2 = sb("n2", [128, G])
        nrm = sb("nrm", [128, G])
        nT = sb("nT", [G, 128])
        nTm = sb("nTm", [G, G, 128])
        lnD = sb("lnD", [128, G * N])
        rD = sb("rD", [128, G * N])
        cosm = sb("cosm", [128, G, N])
        logit = sb("logit", [128, G, N])
        rmax = sb("rmax", [128, G])
        lsh = sb("lsh", [128, G, N])
        pexp = sb("pexp", [128, G, N])
        pT = sb("pT", [128, G, N])
        rsum = sb("rsum", [128, G])
        att = sb("att", [128, G, F])
        x3 = [sb(f"x3_{p}", [128, G, F]) for p in range(2)]
        h4 = [sb(f"h4_{p}", [128, G, F]) for p in range(2)]

        ebuf = [sb(f"ebuf{i}", [128, 1024]) for i in range(2)]
        sbuf1 = [sb(f"sbuf1_{i}", [128, 1024]) for i in range(2)]
        hbuf = [sb(f"hbuf{i}", [128, 1024]) for i in range(2)]
        wbuf = [sb(f"wbuf{i}", [128, 1024]) for i in range(2)]
        t1 = sb("t1", [128, 256, 2])
        t2 = sb("t2", [128, 256, 2])
        prod = [sb(f"prod{p}", [128, 2, QH]) for p in range(2)]
        lq = [sb(f"lq{p}", [128, 2, QH]) for p in range(2)]
        sT = sb("sT", [128, 2, 128])
        sR = sb("sR", [128, G, F])
        osum = sb("osum", [128, G, F])
        ofin = [sb(f"ofin{p}", [128, G, F]) for p in range(2)]

        ps_arg = ctx.enter_context(nc.psum_tensor("ps_arg", [128, 512], F32))
        ps_v1 = ctx.enter_context(nc.psum_tensor("ps_v1", [128, 1024], F32))
        ps_v2 = ctx.enter_context(nc.psum_tensor("ps_v2", [128, 1024], F32))
        ps_rank = ctx.enter_context(nc.psum_tensor("ps_rank", [128, 512], F32))
        ps_a = ctx.enter_context(nc.psum_tensor("ps_a", [128, 512], F32))
        ps_b = ctx.enter_context(nc.psum_tensor("ps_b", [128, 512], F32))
        ps_rank16 = ps_rank[:, 0:256].bitcast(F16)

        consts_in, wz_done = sem("consts_in"), sem("wz_done")
        setup_pe, setup_act, setup_dve = sem("setup_pe"), sem("setup_act"), sem("setup_dve")
        setup_pool = sem("setup_pool")
        adj_in = [sem("adj_in0"), sem("adj_in1")]
        sort_step = sem("sort_step")
        cnt_done, parts_done, diag_done, delta_done, rank_done, perm_done = (
            sem("cnt_done"), sem("parts_done"), sem("diag_done"), sem("delta_done"), sem("rank_done"), sem("perm_done"))
        rows_out = sem("rows_out")
        permT_pe, permT_done, pr_pe, pr_done, rows_in, check_step, neg_done = (
            sem("permT_pe"), sem("permT_done"), sem("pr_pe"), sem("pr_done"), sem("rows_in"), sem("check_step"), sem("neg_done"))
        nz_done, srtc_done, part_step = sem("nz_done"), sem("srtc_done"), sem("part_step")
        arg_done, e_done, v1_done, s1_done, h_done, v2_done, w_done = (
            sem("arg_done"), sem("e_done"), sem("v1_done"), sem("s1_done"), sem("h_done"), sem("v2_done"), sem("w_done"))
        t1_done, t2_done, prod_done, lq_done = sem("t1_done"), sem("t2_done"), sem("prod_done"), sem("lq_done")
        adjT_pe, adjT_done, adj10_done = sem("adjT_pe"), sem("adjT_done"), sem("adj10_done")
        lnA = {k: sem(f"lnA_{k}") for k in ("sum", "xc", "sq", "var", "vareps", "rstd", "h")}
        lnB = {k: sem(f"lnB_{k}") for k in ("sum", "xc", "sq", "var", "vareps", "rstd", "h")}
        hT_pe, hT_done = sem("hT_pe"), sem("hT_done")
        g3_pe, g3_done, g2_pe, g2_done, g1_pe, g1_done, g0_pe, x1_done = (
            sem("g3_pe"), sem("g3_done"), sem("g2_pe"), sem("g2_done"), sem("g1_pe"), sem("g1_done"), sem("g0_pe"), sem("x1_done"))
        rs_done, rsp_done, dpow_done, dinv_done = sem("rs_done"), sem("rsp_done"), sem("dpow_done"), sem("dinv_done")
        hw_pe, y_done, gcn_pe, gcn_done, x2_done = sem("hw_pe"), sem("y_done"), sem("gcn_pe"), sem("gcn_done"), sem("x2_done")
        h2T_pe, h2T_done, nsq_done, n2_done, nrm_done = (
            sem("h2T_pe"), sem("h2T_done"), sem("nsq_done"), sem("n2_done"), sem("nrm_done"))
        nT_pe, nT_done, nTm_done, D_pe, lnD_done, rD_done = (
            sem("nT_pe"), sem("nT_done"), sem("nTm_done"), sem("D_pe"), sem("lnD_done"), sem("rD_done"))
        dots_pe, cos_done, logit_done, rmax_done, lsh_done, pexp_done = (
            sem("dots_pe"), sem("cos_done"), sem("logit_done"), sem("rmax_done"), sem("lsh_done"), sem("pexp_done"))
        pT_pe, pT_done, att_pe, rsum_done, att_done, x3_done = (
            sem("pT_pe"), sem("pT_done"), sem("att_pe"), sem("rsum_done"), sem("att_done"), sem("x3_done"))
        stash_out = sem("stash_out")
        sred_done, stail_step, sT_pe, sR_done, sperm_pe, osum_done, ofin_done = (
            sem("sred_done"), sem("stail_step"), sem("sT_pe"), sem("sR_done"), sem("sperm_pe"), sem("osum_done"), sem("ofin_done"))
        gw_in, gones_done, gd_in, gbc_pe, gsq_done, ge_done, gv1_pe, gv2_pe = (
            sem("gw_in"), sem("gones_done"), sem("gd_in"), sem("gbc_pe"), sem("gsq_done"), sem("ge_done"), sem("gv1_pe"), sem("gv2_pe"))
        gabs_done, gexp_done, gsp_done, gh_done, gw_done, gred_done, gsum_done, gT_pe, grow_done, grow_out = (
            sem("gabs_done"), sem("gexp_done"), sem("gsp_done"), sem("gh_done"), sem("gw_done"), sem("gred_done"), sem("gsum_done"),
            sem("gT_pe"), sem("grow_done"), sem("grow_out"))
        gx_in, gmul_done, gfin_done, gout_out = sem("gx_in"), sem("gmul_done"), sem("gfin_done"), sem("gout_out")
        out_out = [sem("out_out0"), sem("out_out1")]
        flag_pe, flag_dve = sem("flag_pe"), sem("flag_dve")
        TAIL = 1 + sum(s // 4 for _, s, _ in BLOCKS[1:])

        def upto(e, s, v):
            if isinstance(v, int) and v <= 0:
                return
            e.wait_ge(s, v)

        ident = c32s[:, C_ID:C_ID + 128]
        id16 = c16s[:, H_ID:H_ID + 128]

        def ebuf_of(p, c):
            return ebuf[(p + c) % 2]

        def bc(col, n):
            return col.unsqueeze(2).broadcast_to([128, G, n])

        SLOTS = 4 * UNITS
        SORT_STEPS = 2 * (TOP // 8) - 1
        ROWS_DMA = 16 * len(BLOCKS)
        N_CONST = 16 * (2 + G + 10 + 1)

        offs, at = [], 0
        for s0, s, r in BLOCKS:
            offs.append(at)
            at += s * r

        def of(k, p, d=0):
            q = p + d
            return 2 * k + q, k + q // 2, q % 2

        def tile_slice(T):
            return slice(T * G, T * G + G) if isinstance(T, int) else bass.ds(T * G, G)

        def periods(e, period):
            for k in range(2):
                period(k, 0, True, True)
                period(k, 1, True, True)
            with e.Fori(2, NT // 2 - 1) as k:
                period(k, 0, True, True)
                period(k, 1, True, True)
            period(NT // 2 - 1, 0, True, False)
            period(NT // 2 - 1, 1, False, False)

        ROUNDS, STEPS, W = B * 8, 4, 512
        gd = ebuf[0][0:1, :], ebuf[1][0:1, :]
        gsq = hbuf[0]
        ge = hbuf[1]
        gw1 = sbuf1[0][:, 0:F], sbuf1[0][0:KALL - 128, F:2 * F]
        gones = sbuf1[0][0:1, 128:256]
        gabs, grel = sbuf1[1][0:F, 0:W], sbuf1[1][0:F, W:2 * W]
        gexp, glog = wbuf[0][0:F, 0:W], wbuf[0][0:F, W:2 * W]
        gh, gw = wbuf[1][:, 0:W], wbuf[1][0:F, W:2 * W]
        gsum = t1[:, 0:2, :]
        grow = osum[0:4, :, :]
        gx = [x3[0], h4[0]]
        gS = sR

        def loop(e, count, step):
            step(0)
            with e.Fori(1, count) as i:
                step(i)

        def at_index(i):
            return slice(i, i + 1) if isinstance(i, int) else bass.ds(i, 1)

        def general(e, body):
            e.wait_ge(flag_dve, 2)
            flag = e.value_load(flagi[0:1, 0:1])
            with e.If(flag > 0):
                body(e)

        block = ctx.enter_context(nc.Block())

        @block.sync
        def _(sp):
            def load(T, k, p):
                upto(sp, sort_step, SORT_STEPS * (T - 1))
                upto(sp, adjT_pe, T - 1)
                upto(sp, adj10_done, T - 1)
                upto(sp, neg_done, T - 1)
                upto(sp, x1_done, T - 1)
                sp.dma_start(adj_t[p][:, :, :], adj[tile_slice(T)].rearrange("g i j -> i g j")).then_inc(adj_in[p], 16)
                sp.dma_start(x_t[p][:, :, :], x[tile_slice(T)].rearrange("g i f -> i g f")).then_inc(adj_in[p], 16)

            def spread_rows(T, k, p):
                upto(sp, arg_done, UNITS * (T - 1))
                sp.wait_ge(pr_done, 2 * T + 2)
                for (s0, s, r), o in zip(BLOCKS, offs):
                    src = parts_r[0:r, 0:G * PW].rearrange("r (q s) -> r q s", s=TOP)[:, :, s0:s0 + s]
                    dst = rows_dram[p][:, o:o + s * r].rearrange("q (r s) -> r q s", s=s)
                    sp.dma_start(dst, src).then_inc(rows_out, 16)
                sp.wait_ge(rows_out, ROWS_DMA * (T + 1))
                sp.dma_start(argin[p][0:NPART * G, :], rows_dram[p][:, :]).then_inc(rows_in, 16)

            def store_x3(T, k, p):
                sp.wait_ge(x3_done, T + 1)
                sp.wait_ge(lnB["h"], 2 * T + 2)
                dst = scratch[slice(T, T + 1) if isinstance(T, int) else bass.ds(T, 1)].rearrange("o n a f -> (o n) a f")
                sp.dma_start(dst[:, 0, :], x3[p][:, :, :].rearrange("n g f -> n (g f)")).then_inc(stash_out, 16)
                sp.dma_start(dst[:, 1, :], h4[p][:, :, :].rearrange("n g f -> n (g f)")).then_inc(stash_out, 16)

            def store_out(T, k, p):
                sp.wait_ge(ofin_done, T + 1)
                sp.dma_start(out[tile_slice(T)].rearrange("g n f -> n g f"), ofin[p][:, :, :]).then_inc(out_out[p], 16)

            sp.dma_start(c32s[:, :], c32[:, :]).then_inc(consts_in, 16)
            sp.dma_start(c16s[:, :], c16[:, :]).then_inc(consts_in, 16)
            sp.wait_ge(wz_done, 1)
            for g in range(G):
                sp.dma_start(w1z[KF * g:KF * g + KF, g // 2, F * (g % 2):F * (g % 2) + F], w1[0:KF, :]).then_inc(consts_in, 16)
            for g in range(2):
                r = slice(F * g, F * g + F)
                sp.dma_start(w2bd[r, r], w2[:, :]).then_inc(consts_in, 16)
                sp.dma_start(b1c[r, :], b1.rearrange("(f o) -> f o", o=1)).then_inc(consts_in, 16)
                sp.dma_start(b2c[r, :], b2.rearrange("(f o) -> f o", o=1)).then_inc(consts_in, 16)
                sp.dma_start(wks[r, r], wk[:, :]).then_inc(consts_in, 16)
                sp.dma_start(thin[r, :, :], theta.rearrange("k c f -> c k f")).then_inc(consts_in, 16)
            sp.dma_start(betac[:, :], beta.rearrange("(o b) -> o b", o=1).broadcast_to([128, 1])).then_inc(consts_in, 16)
            load(*of(0, 0))
            load(*of(0, 1))
            sp.wait_ge(wz_done, 5)
            spread_rows(*of(0, 0))

            def period(k, p, nxt, nxt2):
                if nxt2:
                    load(*of(k, p, 2))
                if nxt:
                    spread_rows(*of(k, p, 1))
                if not (isinstance(k, int) and k == 0 and p == 0):
                    store_out(*of(k, p, -1))
                store_x3(*of(k, p))

            periods(sp, period)
            store_out(*of(NT // 2 - 1, 1))
            sp.wait_ge(stash_out, 32 * NT)
            for p in range(2):
                sp.wait_ge(out_out[p], 16 * (NT // 2))

            def body(sp):
                sp.dma_start(gw1[0], w1[0:128, :]).then_inc(gw_in, 16)
                sp.dma_start(gw1[1], w1[128:KALL, :]).then_inc(gw_in, 16)
                adj_rounds = adj.rearrange("b (r s) j -> (b r) (s j)", s=16)
                def round_(it):
                    upto(sp, gbc_pe, STEPS * it)
                    src = adj_rounds[at_index(it)]
                    for i in range(2):
                        sp.dma_start(gd[i], src[:, 1024 * i:1024 * i + 1024]).then_inc(gd_in, 16)
                    sp.wait_ge(grow_done, STEPS * it + STEPS)
                    sp.dma_start(s_dram[at_index(it)].rearrange("o s q f -> (o q) s f"), grow).then_inc(grow_out, 16)

                loop(sp, ROUNDS, round_)
                sp.wait_ge(grow_out, 16 * ROUNDS)
                def finish(T):
                    upto(sp, gmul_done, T)
                    upto(sp, gfin_done, T)
                    src = scratch[at_index(T)].rearrange("o n a f -> (o n) a f")
                    for a in range(2):
                        sp.dma_start(gx[a][:, :, :].rearrange("n g f -> n (g f)"), src[:, a, :]).then_inc(gx_in, 16)
                    s_rows = s_dram.rearrange("(b r) s q f -> b (r s q) f", r=8)
                    sp.dma_start(gS[:, :, :], s_rows[tile_slice(T)].rearrange("g n f -> n g f")).then_inc(gx_in, 16)
                    sp.wait_ge(gfin_done, T + 1)
                    sp.dma_start(out[tile_slice(T)].rearrange("g n f -> n g f"), ofin[0][:, :, :]).then_inc(gout_out, 16)

                loop(sp, NT, finish)
                sp.wait_ge(gout_out, 16 * NT)

            general(sp, body)

        @block.gpsimd
        def _(pool):
            pool.memset(w1z[:, :, :], 0.0).then_inc(setup_pool, 1)
            pool.memset(w2bd[:, :], 0.0).then_inc(setup_pool, 1)
            pool.memset(wks[:, :], 0.0).then_inc(setup_pool, 1)
            pool.memset(expo[:, :], -0.5).then_inc(setup_pool, 1)
            pool.memset(half[:, :], 0.5).then_inc(setup_pool, 1)
            pool.memset(ten[:, :], 10.0).then_inc(setup_pool, 1)
            pool.wait_ge(setup_pool, 6)
            pool.memset(onesc[:, :], 1.0).then_inc(wz_done, 1)
            pool.memset(th[:, :, :], 0.0).then_inc(wz_done, 1)
            pool.memset(h2T[:, :, :], 0.0).then_inc(wz_done, 1)
            for p in range(2):
                pool.memset(argin[p][:, :], 0.0).then_inc(wz_done, 1)

            def ln_square(ln, v, a, o):
                pool.wait_ge(ln["xc"], v)
                pool.tensor_tensor(o[:, :, :], a[:, :, :], a[:, :, :], ALU.mult).then_inc(ln["sq"], 1)

            def ln_power(ln, v, a, o):
                pool.wait_ge(ln["vareps"], v)
                pool.tensor_tensor(o[:, :], a[:, :], expo[:, :], ALU.pow).then_inc(ln["rstd"], 1)

            def count_diag(T, k, p):
                pool.wait_ge(cnt_done, T + 1)
                upto(pool, delta_done, T)
                pool.tensor_tensor(diag[:, :, :], id16.unsqueeze(1).broadcast_to([128, G, 128]), bc(cnt[:, :], 128),
                                   ALU.mult).then_inc(diag_done, 1)

            def adj_times_10(T, k, p):
                pool.wait_ge(adj_in[p], 32 * (k + 1))
                upto(pool, logit_done, T - 1)
                pool.tensor_tensor(adj10[p][:, :, :], adj_t[p][:, :, :], ten[:, :].unsqueeze(2).broadcast_to([128, G, N]), ALU.mult)\
                    .then_inc(adj10_done, 1)

            def degree_power(T, k, p):
                pool.wait_ge(rsp_done, 2 * T + 2)
                pool.tensor_tensor(dinv0[:, :], rsp[:, :], expo[:, :], ALU.pow).then_inc(dpow_done, 1)

            def norm_square(T, k, p):
                pool.wait_ge(lnB["h"], 2 * T + 1)
                pool.tensor_tensor(sq2[:, :, :], h2[:, :, :], h2[:, :, :], ALU.mult).then_inc(nsq_done, 1)

            def norm_power(T, k, p):
                pool.wait_ge(n2_done, T + 1)
                pool.tensor_tensor(nrm[:, :], n2[:, :], half[:, :], ALU.pow).then_inc(nrm_done, 1)

            def close_sums(T, k, p):
                pool.wait_ge(sred_done, T + 1)
                pool.tensor_tensor(sT[:, :, :], sT[:, :, :], kmat[:, :, :], ALU.add).then_inc(stail_step, 1)
                n = 1
                for (s0, s, r), o in list(zip(BLOCKS, offs))[1:]:
                    for j in range(s // 4):
                        v = lq[p][:, :, o // 4:o // 4 + r * s // 4].rearrange("k h (r j) -> k h r j", j=s // 4)[:, :, :, j]
                        pool.wait_ge(stail_step, TAIL * T + n)
                        pool.tensor_tensor(sT[:, :, 0:r], sT[:, :, 0:r], v, ALU.add).then_inc(stail_step, 1)
                        n += 1
                assert n == TAIL

            t0 = of(0, 0)
            count_diag(*t0)
            ln_square(lnA, 1, xc, sq)
            ln_power(lnA, 1, var, rstd)
            adj_times_10(*t0)
            ln_square(lnA, 2, xc, sq)
            degree_power(*t0)
            ln_power(lnA, 2, var, rstd)

            def period(k, p, nxt, nxt2):
                t, k0, p0 = of(k, p)
                n = of(k, p, 1)
                if nxt:
                    count_diag(*n)
                    ln_square(lnA, 2 * t + 3, xc, sq)
                ln_square(lnB, 2 * t + 1, xc2, sq2)
                if nxt:
                    ln_power(lnA, 2 * t + 3, var, rstd)
                ln_power(lnB, 2 * t + 1, var2, rstd2)
                if nxt:
                    adj_times_10(*n)
                norm_square(t, k0, p0)
                norm_power(t, k0, p0)
                if not (isinstance(k, int) and k == 0 and p == 0):
                    close_sums(*of(k, p, -1))
                if nxt:
                    ln_square(lnA, 2 * t + 4, xc, sq)
                    degree_power(*n)
                    ln_power(lnA, 2 * t + 4, var, rstd)
                ln_square(lnB, 2 * t + 2, xc2, sq2)
                ln_power(lnB, 2 * t + 2, var2, rstd2)

            periods(pool, period)
            close_sums(*of(NT // 2 - 1, 1))

        @block.scalar
        def _(act):
            act.preload_act_table_set("natural_log_exp_and_others")
            act.wait_ge(consts_in, N_CONST)
            act.activation(setup[:, 0:1], c32s[:, C_BIAS:C_BIAS + 1], ACT.Exp).then_inc(setup_act, 1)
            act.wait_ge(setup_dve, 3)
            act.activation(setup[:, 1:4], setup[:, 1:4], ACT.Exp).then_inc(setup_act, 1)
            act.wait_ge(setup_act, 2)
            act.activation(setup[:, 4:7], setup[:, 1:4], ACT.Ln, bias=1.0).then_inc(setup_act, 1)
            act.wait_ge(setup_dve, 4)
            act.activation(setup[:, 9:10], setup[:, 8:9], ACT.Exp).then_inc(setup_act, 1)
            act.wait_ge(setup_act, 4)
            act.activation(setup[:, 10:11], setup[:, 9:10], ACT.Ln, bias=1.0).then_inc(setup_act, 1)

            def rbf(t, p, j):
                c = j // 2
                act.wait_ge(arg_done, 9 * t + j + 1)
                upto(act, v1_done, 9 * t + (c - 1 if c < 2 else 2 * c - 2))
                act.activation(ebuf_of(p, c)[:, 512 * (j % 2):512 * (j % 2) + 512], ps_arg[:, :], ACT.Exp,
                               bias=c32s[:, C_BIAS:C_BIAS + 1]).then_inc(e_done, 1)

            def exp1(t, u, q):
                act.wait_ge(v1_done, 9 * t + u + 1)
                act.activation(sbuf1[q][:, :], ps_v1[:, :], ACT.Exp, bias=b1c[:, 0:1]).then_inc(s1_done, 1)

            def log1(t, u, q):
                act.wait_ge(s1_done, 9 * t + u + 1)
                upto(act, v2_done, 9 * t + u - 1)
                act.activation(hbuf[q][:, :], sbuf1[q][:, :], ACT.Ln, bias=1.0).then_inc(h_done, 1)

            def exp2(t, u, q):
                act.wait_ge(v2_done, 9 * t + u + 1)
                upto(act, t2_done, 9 * t + u - 1)
                act.activation(wbuf[q][:, :], ps_v2[:, :], ACT.Exp, bias=b2p[:, 0:1]).then_inc(w_done, 1)

            def log2(T, k, p, i):
                act.wait_ge(prod_done, 9 * T + (4, 6, 9)[i])
                upto(act, sred_done, T - 1)
                upto(act, stail_step, TAIL * (T - 1))
                r = slice(i * QP, i * QP + QP)
                act.activation(lq[p][:, :, r], prod[p][:, :, r], ACT.Ln).then_inc(lq_done, 1)

            def copy_adjT(T, k, p):
                act.wait_ge(adjT_pe, T + 1)
                upto(act, gcn_pe, T)
                act.copy(adj_tr[:, :, :].rearrange("n g m -> n (g m)"), ps_a[:, :]).then_inc(adjT_done, 1)

            def negatives(T, k, p):
                act.wait_ge(adj_in[p], 32 * (k + 1))
                upto(act, check_step, 4 * T)
                act.activation(junka[:, :], adj_t[p][:, :, :].rearrange("n g m -> n (g m)"), ACT.Relu, scale=-1.0,
                               accum_out=badneg[:, 0:1]).then_inc(neg_done, 1)

            def copy_hT(T, j):
                act.wait_ge(hT_pe, 2 * T + j + 1)
                act.copy(hT[:, :, :].rearrange("n g m -> n (g m)"), ps_a[:, 0:256]).then_inc(hT_done, 1)

            def twice_b3(T, k, p):
                act.wait_ge(g3_pe, T + 1)
                act.mul(b3x2[:, :, :].rearrange("n g m -> n (g m)"), ps_a[:, 0:256], 2.0).then_inc(g3_done, 1)

            def twice_b2(T, k, p):
                act.wait_ge(g2_pe, T + 1)
                act.mul(b2x2[:, :, :].rearrange("n g m -> n (g m)"), ps_a[:, 0:256], 2.0).then_inc(g2_done, 1)

            def copy_ranked(T, k, p, j):
                act.wait_ge(pr_pe, 2 * T + j + 1)
                upto(act, rows_out, ROWS_DMA * T)
                upto(act, check_step, 4 * T)
                act.copy(parts_r[:, 2 * PW * j:2 * PW * j + 2 * PW], ps_rank[:, 0:2 * PW])
                act.copy(parts_r[:, G * PW + 2 * j:G * PW + 2 * j + 2], ps_rank[:, 2 * PW:2 * PW + 2]).then_inc(pr_done, 1)

            def copy_permT(T, k, p):
                act.wait_ge(permT_pe, T + 1)
                upto(act, sperm_pe, T - 1)
                act.copy(perm_t[p][:, :, :].rearrange("r g n -> r (g n)"), ps_rank16).then_inc(permT_done, 1)

            def copy_h2T(T, k, p):
                act.wait_ge(h2T_pe, T + 1)
                upto(act, dots_pe, T)
                for e in range(2):
                    m = act.copy(h2T[64 * e:64 * e + 64, e::2, :],
                                 ps_b[64 * e:64 * e + 64, 0:256].rearrange("f (h n) -> f h n", h=2))
                m.then_inc(h2T_done, 1)

            def copy_nT(T, k, p):
                act.wait_ge(nT_pe, T + 1)
                act.copy(nT[:, :], ps_b[0:G, 0:128]).then_inc(nT_done, 1)

            def log_D(T, k, p):
                act.wait_ge(D_pe, T + 1)
                act.activation(lnD[:, :], ps_b[:, :], ACT.Ln, bias=epsc[:, 0:1]).then_inc(lnD_done, 1)

            def recip_D(T, k, p):
                act.wait_ge(lnD_done, T + 1)
                act.activation(rD[:, :], lnD[:, :], ACT.Exp, scale=-1.0).then_inc(rD_done, 1)

            def exp_logits(T, k, p):
                act.wait_ge(lsh_done, T + 1)
                upto(act, pT_pe, T)
                act.activation(pexp[:, :, :], lsh[:, :, :], ACT.Exp).then_inc(pexp_done, 1)

            def copy_pT(T, k, p):
                act.wait_ge(pT_pe, T + 1)
                act.copy(pT[:, :, :].rearrange("n g m -> n (g m)"), ps_b[:, :]).then_inc(pT_done, 1)

            def copy_sR(T, k, p):
                act.wait_ge(sT_pe, T + 1)
                act.copy(sR[:, :, :].rearrange("n g m -> n (g m)"), ps_rank[:, 0:256]).then_inc(sR_done, 1)

            t0 = of(0, 0)
            copy_adjT(*t0)
            negatives(*t0)
            copy_hT(0, 0)
            twice_b3(*t0)
            twice_b2(*t0)
            for j in range(2):
                copy_ranked(*t0, j)
            copy_permT(*t0)
            copy_hT(0, 1)
            rbf(0, 0, 0)
            rbf(0, 0, 1)

            def period(k, p, nxt, nxt2):
                t, k0, p0 = of(k, p)
                n = of(k, p, 1)
                c = of(k, p)
                b = of(k, p, -1)
                first = isinstance(k, int) and k == 0 and p == 0
                def steps(slot):
                    def at(name, f, *a):
                        if ACT_AT[name] == slot:
                            f(*a)

                    if nxt:
                        at("copy_adjT", copy_adjT, *n)
                        at("negatives", negatives, *n)
                        at("copy_hT0", copy_hT, n[0], 0)
                        at("copy_ranked0", copy_ranked, *n, 0)
                        at("copy_ranked1", copy_ranked, *n, 1)
                        at("twice_b3", twice_b3, *n)
                        at("twice_b2", twice_b2, *n)
                        at("copy_hT1", copy_hT, n[0], 1)
                    if not first:
                        at("log22", log2, *b, 2)
                        at("copy_sR", copy_sR, *b)
                    if nxt:
                        at("copy_permT", copy_permT, *n)
                    at("copy_h2T", copy_h2T, *c)
                    at("copy_nT", copy_nT, *c)
                    at("log_D", log_D, *c)
                    at("recip_D", recip_D, *c)
                    at("log20", log2, *c, 0)
                    at("exp_logits", exp_logits, *c)
                    at("copy_pT", copy_pT, *c)
                    at("log21", log2, *c, 1)

                for u in range(UNITS):
                    exp1(t, u, (p + u) % 2)
                    steps(4 * u)
                    if u + 2 < UNITS:
                        rbf(t, p, u + 2)
                    elif nxt:
                        rbf(t + 1, 1 - p, u + 2 - UNITS)
                    steps(4 * u + 1)
                    if not (first and u == 0):
                        exp2(t if u else t - 1, (u - 1) % UNITS, (p + u - 1) % 2)
                    steps(4 * u + 2)
                    log1(t, u, (p + u) % 2)
                    steps(4 * u + 3)

            periods(act, period)
            exp2(NT - 1, UNITS - 1, (1 + UNITS - 1) % 2)
            log2(*of(NT // 2 - 1, 1), 2)
            copy_sR(*of(NT // 2 - 1, 1))

            def softplus(act, ps, bias, v):
                act.activation(gabs, ps, ACT.Abs, bias=bias[0:F, 0:1]).then_inc(gabs_done, 1)
                act.activation(grel, ps, ACT.Relu, bias=bias[0:F, 0:1])
                act.wait_ge(gabs_done, v)
                act.activation(gexp, gabs, ACT.Exp, scale=-1.0).then_inc(gexp_done, 1)
                act.wait_ge(gexp_done, v)
                act.activation(glog, gexp, ACT.Ln, bias=1.0).then_inc(gsp_done, 1)

            def body(act):
                def round_(it):
                    for s in range(STEPS):
                        n = STEPS * it + s
                        act.wait_ge(gbc_pe, n + 1)
                        act.activation(gsq[:, 0:W], ps_v1[:, 0:W], ACT.Square, bias=c32s[:, C_CEN:C_CEN + 1])
                        act.activation(gsq[0:KALL - 128, W:2 * W], ps_v1[0:KALL - 128, 0:W], ACT.Square,
                                       bias=c32s[0:KALL - 128, C_CEN + 1:C_CEN + 2]).then_inc(gsq_done, 1)
                        act.wait_ge(gsq_done, n + 1)
                        act.activation(ge[:, 0:W], gsq[:, 0:W], ACT.Exp, scale=-GAMMA)
                        act.activation(ge[0:KALL - 128, W:2 * W], gsq[0:KALL - 128, W:2 * W], ACT.Exp, scale=-GAMMA)\
                            .then_inc(ge_done, 1)
                        act.wait_ge(gv1_pe, n + 1)
                        softplus(act, ps_v2[0:F, 0:W], b1c, 2 * n + 1)
                        act.wait_ge(gv2_pe, n + 1)
                        softplus(act, ps_v2[0:F, W:2 * W], b2p, 2 * n + 2)
                        act.wait_ge(gT_pe, n + 1)
                        if s == 0:
                            upto(act, grow_out, 16 * it)
                        act.copy(grow[:, s, :], ps_a[0:4, 0:F]).then_inc(grow_done, 1)

                loop(act, ROUNDS, round_)

            general(act, body)

        @block.tensor
        def _(pe):
            pe.wait_ge(consts_in, N_CONST)
            pe.wait_ge(setup_dve, 1)
            pe.wait_ge(setup_act, 1)
            emax = c32s[:, C_EMAX:C_EMAX + 1]
            pe.matmul(ps_a[:, 0:1], w1z[:, 0, :], setup[:, 0:1], start=True, stop=True)
            pe.matmul(ps_a[:, 1:2], wpos1[:, :], emax, start=True, stop=True)
            pe.matmul(ps_a[:, 2:3], wneg1[:, :], emax, start=True, stop=True)
            pe.matmul(ps_a[:, 3:4], w2bd[:, :], c32s[:, C_NLOG:C_NLOG + 1], start=True, stop=True).then_inc(setup_pe, 1)
            pe.wait_ge(setup_act, 3)
            pe.matmul(ps_b[:, 0:1], w2bd[:, :], setup[:, 4:5], start=True, stop=True)
            pe.matmul(ps_b[:, 1:2], wpos2[:, :], setup[:, 5:6], start=True, stop=False)
            pe.matmul(ps_b[:, 1:2], wneg2[:, :], setup[:, 6:7], start=False, stop=True).then_inc(setup_pe, 1)
            pe.wait_ge(setup_dve, 4)

            def arg(t, j, p):
                if j == 0:
                    pe.wait_ge(rows_in, 16 * (t + 1))
                upto(pe, e_done, 9 * t + j)
                pe.matmul(ps_arg[:, :], c16s[:, H_ARGW:H_ARGW + 128],
                          argin[p][:, 512 * j:512 * j + 512], start=True, stop=True).then_inc(arg_done, 1)

            def layer1(t, p, u, i):
                c, h = u // 2, u % 2
                e = ebuf_of(p, c)
                if i == 0:
                    pe.wait_ge(e_done, 9 * t + min(2 * c + 2, UNITS))
                    upto(pe, s1_done, 9 * t + u)
                pair, cols = (h, slice(512 * i, 512 * i + 512)) if u < UNITS - 1 else (i, slice(0, 512))
                m = pe.matmul(ps_v1[:, 512 * i:512 * i + 512], w1z[:, pair, :], e[:, cols], start=True, stop=True)
                if i == 1:
                    m.then_inc(v1_done, 1)

            def layer2(t, u, q, i):
                if i == 0:
                    pe.wait_ge(h_done, 9 * t + u + 1)
                    upto(pe, w_done, 9 * t + u)
                r = slice(512 * i, 512 * i + 512)
                m = pe.matmul(ps_v2[:, r], w2bd[:, :], hbuf[q][:, r], start=True, stop=True)
                if i == 1:
                    m.then_inc(v2_done, 1)

            def adjT(T, k, p):
                pe.wait_ge(adj_in[p], 32 * (k + 1))
                upto(pe, gcn_done, T)
                for g in range(G):
                    m = pe.transpose(ps_a[:, 128 * g:128 * g + 128], adj_t[p][:, g, :], ident)
                m.then_inc(adjT_pe, 1)

            def hT_(T, j):
                pe.wait_ge(lnA["h"], 2 * T + j + 1)
                if j == 0:
                    pe.wait_ge(adjT_done, T + 1)
                else:
                    pe.wait_ge(rsp_done, 2 * T + 2)
                for h in range(2):
                    m = pe.transpose(ps_a[:, 128 * h:128 * h + 128],
                                     hcur[:, 2 * h:2 * h + 2, :].rearrange("n g f -> n (g f)"), ident)
                m.then_inc(hT_pe, 1)

            def feat(h, w, stop):
                return pe.matmul(ps_a[:, 128 * h:128 * h + 128], hT[:, h, :], w, start=True, stop=stop)

            def cheb(T, order, rhs, done, v, signal):
                pe.wait_ge(done, v)
                for h in range(2):
                    m = feat(h, th[:, order, :], rhs is None)
                    if rhs is not None:
                        for g in (2 * h, 2 * h + 1):
                            m = pe.matmul(ps_a[:, F * g:F * g + F], adj_tr[:, g, :], rhs[:, g, :], start=False, stop=g % 2 == 1)
                m.then_inc(signal, 1)

            def row_sums(T, k, p):
                pe.wait_ge(x1_done, T + 1)
                for g in range(G):
                    m = pe.matmul(ps_a[:, g:g + 1], adj_tr[:, g, :], onesc[:, :], start=True, stop=True)
                m.then_inc(rs_done, 1)

            def hw(T, k, p):
                pe.wait_ge(hT_done, 2 * T + 2)
                for h in range(2):
                    m = feat(h, wks[:, :], True)
                m.then_inc(hw_pe, 1)

            def gcn_mm(T, k, p):
                pe.wait_ge(y_done, T + 1)
                for g in range(G):
                    pe.matmul(ps_a[:, F * g:F * g + F], adj_tr[:, g, :], ysc[:, g, :], start=True, stop=False)
                    m = pe.matmul(ps_a[:, F * g:F * g + F], ident, ysc[:, g, :], start=False, stop=True)
                m.then_inc(gcn_pe, 1)

            def delta(T, k, p):
                pe.wait_ge(diag_done, T + 1)
                upto(pe, permT_done, T)
                for g in range(G):
                    o = ps_rank[:, 128 * g:128 * g + 128]
                    pe.matmul(o, id16, c16s[:, H_CMAT:H_CMAT + 128], start=True, stop=False)
                    pe.matmul(o, c16s[:, H_P128:H_P128 + 128], diag[:, g, :], start=False, stop=False)
                    m = pe.matmul(o, diag[:, g, :], c16s[:, H_N128:H_N128 + 128], start=False, stop=True)
                m.then_inc(delta_done, 1)

            def rank_parts(T, k, p, j):
                pe.wait_ge(perm_done, T + 1)
                pe.wait_ge(parts_done, T + 1)
                if j:
                    pe.wait_ge(pr_done, 2 * T + 1)
                for i in range(2):
                    g = 2 * j + i
                    pe.matmul(ps_rank[:, PW * i:PW * i + PW], perm[:, g, :], parts[:, PW * g:PW * g + PW],
                              start=True, stop=True)
                    m = pe.matmul(ps_rank[:, 2 * PW + i:2 * PW + i + 1], perm[:, g, :],
                                  parts[:, G * PW + g:G * PW + g + 1], start=True, stop=True)
                m.then_inc(pr_pe, 1)

            def permT(T, k, p):
                pe.wait_ge(pr_done, 2 * T + 2)
                upto(pe, osum_done, T - 1)
                for g in range(G):
                    m = pe.transpose(ps_rank16[:, 128 * g:128 * g + 128], perm[:, g, :], id16)
                m.then_inc(permT_pe, 1)

            def sT_mm(T, k, p, ranked):
                pe.wait_ge(stail_step, TAIL * (T + 1))
                pe.wait_ge(permT_done, T + 2 if ranked else T + 1)
                if ranked:
                    pe.wait_ge(pr_done, 2 * T + 6)
                for h in range(2):
                    m = pe.transpose(ps_rank[:, 128 * h:128 * h + 128], sT[:, h, :], ident)
                m.then_inc(sT_pe, 1)

            def sperm(T, k, p):
                pe.wait_ge(sR_done, T + 1)
                for g in range(G):
                    m = pe.matmul(ps_rank[:, F * g:F * g + F], perm_t[p][:, g, :], sR[:, g, :], start=True, stop=True)
                m.then_inc(sperm_pe, 1)

            def h2T_mm(T, k, p):
                pe.wait_ge(lnB["h"], 2 * T + 1)
                upto(pe, att_done, T)
                for h in range(2):
                    m = pe.transpose(ps_b[:, 128 * h:128 * h + 128], h2[:, 2 * h:2 * h + 2, :].rearrange("n g f -> n (g f)"), ident)
                m.then_inc(h2T_pe, 1)

            def nT_mm(T, k, p):
                pe.wait_ge(nrm_done, T + 1)
                pe.wait_ge(h2T_done, T + 1)
                pe.transpose(ps_b[0:G, 0:128], nrm[:, :], ident).then_inc(nT_pe, 1)

            def D_mm(T, k, p):
                pe.wait_ge(nTm_done, T + 1)
                pe.matmul(ps_b[:, :], nT[:, :], nTm[:, :, :].rearrange("b g m -> b (g m)"), start=True, stop=True)\
                    .then_inc(D_pe, 1)

            def dots(T, k, p):
                pe.wait_ge(lnD_done, T + 1)
                for g in range(G):
                    m = pe.matmul(ps_b[:, 128 * g:128 * g + 128], h2T[:, g, :], h2T[:, g, :], start=True, stop=True)
                m.then_inc(dots_pe, 1)

            def pT_mm(T, k, p):
                pe.wait_ge(pexp_done, T + 1)
                for g in range(G):
                    m = pe.transpose(ps_b[:, 128 * g:128 * g + 128], pexp[:, g, :], ident)
                m.then_inc(pT_pe, 1)

            def att_mm(T, k, p):
                pe.wait_ge(pT_done, T + 1)
                for g in range(G):
                    pe.matmul(ps_b[:, F * g:F * g + F], pT[:, g, :], h2[:, g, :], start=True, stop=True)
                    m = pe.matmul(ps_b[:, F * G + g:F * G + g + 1], pT[:, g, :], onesc[:, :], start=True, stop=True)
                m.then_inc(att_pe, 1)

            t0 = of(0, 0)
            adjT(*t0)
            hT_(0, 0)
            cheb(0, 3, None, hT_done, 1, g3_pe)
            cheb(0, 2, b3x2, g3_done, 1, g2_pe)
            cheb(0, 1, b2x2, g2_done, 1, g1_pe)
            cheb(0, 0, d1, g1_done, 1, g0_pe)
            row_sums(*t0)
            delta(*t0)
            rank_parts(*t0, 0)
            rank_parts(*t0, 1)
            permT(*t0)
            hT_(0, 1)
            hw(*t0)
            gcn_mm(*t0)
            arg(0, 0, 0)
            arg(0, 1, 0)
            arg(0, 2, 0)
            layer1(0, 0, 0, 0)
            layer1(0, 0, 0, 1)

            def period(k, p, nxt, nxt2):
                t, k0, p0 = of(k, p)
                n = of(k, p, 1)
                c = of(k, p)
                b = of(k, p, -1)
                first = isinstance(k, int) and k == 0 and p == 0
                def steps(slot):
                    def at(name, f, *a):
                        if PE_AT[name] == slot:
                            f(*a)

                    if nxt:
                        T = n[0]
                        at("adjT", adjT, *n)
                        at("delta", delta, *n)
                        at("hT0", hT_, T, 0)
                        at("rank_parts0", rank_parts, *n, 0)
                        at("cheb3", cheb, T, 3, None, hT_done, 2 * T + 1, g3_pe)
                        at("rank_parts1", rank_parts, *n, 1)
                        at("cheb2", cheb, T, 2, b3x2, g3_done, T + 1, g2_pe)
                        at("cheb1", cheb, T, 1, b2x2, g2_done, T + 1, g1_pe)
                        at("cheb0", cheb, T, 0, d1, g1_done, T + 1, g0_pe)
                        at("row_sums", row_sums, *n)
                        at("hT1", hT_, T, 1)
                        at("hw", hw, *n)
                        at("gcn_mm", gcn_mm, *n)
                    if not first:
                        at("sT_mm", sT_mm, *b, nxt)
                        at("sperm", sperm, *b)
                    if nxt:
                        at("permT", permT, *n)
                    at("h2T_mm", h2T_mm, *c)
                    at("nT_mm", nT_mm, *c)
                    at("D_mm", D_mm, *c)
                    at("dots", dots, *c)
                    at("pT_mm", pT_mm, *c)
                    at("att_mm", att_mm, *c)

                for u in range(UNITS):
                    for i in range(2):
                        if u < UNITS - 1:
                            layer1(t, p, u + 1, i)
                        elif nxt:
                            layer1(t + 1, 1 - p, 0, i)
                        if i == 1:
                            if u + 3 < UNITS:
                                arg(t, u + 3, p)
                            elif nxt:
                                arg(t + 1, u + 3 - UNITS, 1 - p)
                        steps(4 * u + i)
                    for i in range(2):
                        layer2(t, u, (p + u) % 2, i)
                        steps(4 * u + 2 + i)

            periods(pe, period)
            sT_mm(*of(NT // 2 - 1, 1), False)
            sperm(*of(NT // 2 - 1, 1))
            pe.wait_ge(osum_done, NT)
            pe.wait_ge(check_step, 4 * NT)
            pe.transpose(ps_a[0:1, 0:128], bad[:, :], ident).then_inc(flag_pe, 1)

            def body(pe):
                pe.wait_ge(gw_in, 32)
                pe.wait_ge(gones_done, 1)
                def round_(it):
                    pe.wait_ge(gd_in, 32 * it + 32)
                    for s in range(STEPS):
                        n = STEPS * it + s
                        upto(pe, gsq_done, n)
                        pe.matmul(ps_v1[:, 0:W], gones, gd[s // 2][:, W * (s % 2):W * (s % 2) + W], start=True, stop=True)\
                            .then_inc(gbc_pe, 1)
                        pe.wait_ge(ge_done, n + 1)
                        upto(pe, gsp_done, 2 * n)
                        pe.matmul(ps_v2[0:F, 0:W], gw1[0], ge[:, 0:W], start=True, stop=False)
                        pe.matmul(ps_v2[0:F, 0:W], gw1[1], ge[0:KALL - 128, W:2 * W], start=False, stop=True).then_inc(gv1_pe, 1)
                        pe.wait_ge(gh_done, n + 1)
                        pe.matmul(ps_v2[:, W:2 * W], w2bd[:, :], gh, start=True, stop=True).then_inc(gv2_pe, 1)
                        pe.wait_ge(gsum_done, n + 1)
                        upto(pe, grow_done, n)
                        pe.transpose(ps_a[0:4, 0:128], gsum.rearrange("f a b -> f (a b)"), ident).then_inc(gT_pe, 1)

                loop(pe, ROUNDS, round_)

            general(pe, body)

        @block.vector
        def _(dve):
            dve.wait_ge(consts_in, N_CONST)
            dve.memset(epsc[:, :], EPS_COS)
            dve.tensor_scalar(wpos1[:, :], w1z[:, 0, :], 0.0, None, ALU.max)
            dve.tensor_scalar(wneg1[:, :], w1z[:, 0, :], 0.0, None, ALU.min)
            dve.tensor_scalar(wpos2[:, :], w2bd[:, :], 0.0, None, ALU.max)
            dve.tensor_scalar(wneg2[:, :], w2bd[:, :], 0.0, None, ALU.min)
            dve.wait_ge(wz_done, 5)
            for e in range(2):
                r = slice(F * e, F * e + F)
                dve.tensor_copy(th[r, 2:4, r], thin[r, 2:4, :])
                m = dve.tensor_tensor(th[r, 0:2, r], thin[r, 0:2, :], thin[r, 2:4, :], ALU.subtract)
            m.then_inc(setup_dve, 1)
            dve.wait_ge(setup_pe, 1)
            dve.tensor_scalar(b2p[:, :], ps_a[:, 3:4], b2c[:, 0:1], None, ALU.add).then_inc(setup_dve, 1)
            dve.tensor_scalar(setup[:, 7:8], ps_a[:, 1:2], b1c[:, 0:1], 40.0, ALU.add, ALU.subtract)
            dve.tensor_scalar(setup[:, 1:4], ps_a[:, 0:3], b1c[:, 0:1], 60.0, ALU.add, ALU.min).then_inc(setup_dve, 1)
            dve.wait_ge(setup_pe, 2)
            dve.wait_ge(setup_dve, 3)
            dve.tensor_scalar(setup[:, 11:12], ps_b[:, 1:2], b2p[:, 0:1], 10.0, ALU.add, ALU.subtract)
            dve.tensor_scalar(setup[:, 8:9], ps_b[:, 0:1], b2p[:, 0:1], 60.0, ALU.add, ALU.min).then_inc(setup_dve, 1)
            dve.wait_ge(setup_dve, 4)
            dve.tensor_tensor(bad[:, :], setup[:, 7:8], setup[:, 11:12], ALU.max).then_inc(setup_dve, 1)
            dve.wait_ge(setup_act, 5)
            for h in range(2):
                m = dve.tensor_scalar(kmat[:, h, :], c32s[:, C_MISS:C_MISS + 128], setup[:, 10:11], -N * LOG2,
                                      ALU.mult, ALU.add)
            m.then_inc(setup_dve, 1)
            dve.wait_ge(setup_dve, 6)

            def sort_max(T, k, p, r):
                if r == 0:
                    dve.wait_ge(adj_in[p], 32 * (k + 1))
                else:
                    dve.wait_ge(sort_step, SORT_STEPS * T + 2 * r)
                dve.memset(gate[:, :], 0.0)
                for g in range(G):
                    m = dve.max(srt[:, g, 8 * r:8 * r + 8], (srt_w if r else adj_t[p])[:, g, :])
                m.then_inc(sort_step, 1)

            def sort_remove(T, k, p, r):
                dve.wait_ge(sort_step, SORT_STEPS * T + 2 * r + 1)
                dve.memset(gate[:, :], 0.0)
                for g in range(G):
                    m = dve.match_replace(srt_w[:, g, :], srt[:, g, 8 * r:8 * r + 8], (srt_w if r else adj_t[p])[:, g, :], 0.0)
                m.then_inc(sort_step, 1)

            def sort_round(T, k, p, r):
                sort_max(T, k, p, r)
                if r < TOP // 8 - 1:
                    sort_remove(T, k, p, r)

            def counts(T, k, p):
                dve.wait_ge(sort_step, SORT_STEPS * (T + 1))
                upto(dve, diag_done, T)
                dve.tensor_scalar(nz[:, :, :], srt[:, :, :], 0.0, None, ALU.not_equal).then_inc(nz_done, 1)
                dve.tensor_scalar(srt_c[:, :, :], srt[:, :, :], 0.25, -0.25, ALU.min, ALU.max).then_inc(srtc_done, 1)
                dve.wait_ge(nz_done, T + 1)
                dve.tensor_reduce(cnt[:, :], nz[:, :, :], AX.X, ALU.add).then_inc(cnt_done, 1)

            def split_parts(T, k, p):
                def col(q):
                    return parts[:, 0:G * PW].rearrange("n (g w) -> n g w", g=G)[:, :, TOP * q:TOP * q + TOP]
                upto(dve, pr_pe, 2 * T)
                dve.wait_ge(srtc_done, T + 1)
                dve.tensor_tensor(dsq[:, :, :], srt_c[:, :, :], srt_c[:, :, :], ALU.mult).then_inc(part_step, 1)
                dve.tensor_scalar(col(0), srt_c[:, :, :], DSCALE, None, ALU.mult).then_inc(part_step, 1)
                dve.wait_ge(cnt_done, T + 1)
                dve.tensor_copy(parts[:, G * PW:G * PW + G], cnt[:, :])
                dve.wait_ge(part_step, 3 * T + 2)
                dve.tensor_scalar(col(2), dsq[:, :, :], QSCALE, None, ALU.mult).then_inc(part_step, 1)
                dve.scalar_tensor_tensor(out=col(1), in0=srt_c[:, :, :], scalar=DSCALE, in1=col(0),
                                         op0=ALU.mult, op1=ALU.subtract)
                dve.wait_ge(part_step, 3 * T + 3)
                dve.scalar_tensor_tensor(out=col(3), in0=dsq[:, :, :], scalar=QSCALE, in1=col(2),
                                         op0=ALU.mult, op1=ALU.subtract).then_inc(parts_done, 1)

            def check_sorted(T, k, p):
                upto(dve, check_step, 4 * T)
                dve.tensor_scalar(junk4[:, :], srt[:, :, TOP - 1], 1.0, bad[:, 0:1], ALU.mult, ALU.max,
                                  accum_out=bad[:, 0:1]).then_inc(check_step, 1)
                dve.wait_ge(check_step, 4 * T + 1)
                dve.tensor_scalar(junk4[:, :], srt[:, :, 0], DMAX, bad[:, 0:1], ALU.subtract, ALU.max,
                                  accum_out=bad[:, 0:1]).then_inc(check_step, 1)

            def check_ranked(T, k, p):
                dve.wait_ge(pr_done, 2 * T + 2)
                dve.wait_ge(check_step, 4 * T + 2)
                dve.tensor_scalar(junk4[:, :], parts_r[:, G * PW:G * PW + G], c32s[:, C_CAP:C_CAP + 1], bad[:, 0:1],
                                  ALU.subtract, ALU.max, accum_out=bad[:, 0:1]).then_inc(check_step, 1)
                dve.wait_ge(check_step, 4 * T + 3)
                dve.wait_ge(neg_done, T + 1)
                dve.tensor_tensor(bad[:, :], bad[:, :], badneg[:, :], ALU.max).then_inc(check_step, 1)

            def ranks(T, k, p):
                dve.wait_ge(delta_done, T + 1)
                for g in range(G):
                    m = dve.tensor_scalar(junk[:, g, :], ps_rank[:, 128 * g:128 * g + 128], 0.0, None, ALU.is_gt, ALU.add,
                                          accum_out=rank[:, g:g + 1])
                m.then_inc(rank_done, 1)

            def perms(T, k, p):
                dve.wait_ge(rank_done, T + 1)
                upto(dve, permT_pe, T)
                for g in range(G):
                    m = dve.tensor_scalar(perm[:, g, :], c16s[:, H_IOTA:H_IOTA + 128], rank[:, g:g + 1], None, ALU.is_equal)
                m.then_inc(perm_done, 1)

            def ln_centre(ln, v, src, s, xo):
                dve.tensor_reduce(s[:, :], src[:, :, :], AX.X, ALU.add).then_inc(ln["sum"], 1)
                dve.wait_ge(ln["sum"], v)
                dve.scalar_tensor_tensor(out=xo[:, :, :], in0=bc(s[:, :], F), scalar=-1.0 / F, in1=src[:, :, :],
                                         op0=ALU.mult, op1=ALU.add).then_inc(ln["xc"], 1)

            def ln_var(ln, v, sqr, o):
                dve.wait_ge(ln["sq"], v)
                dve.tensor_reduce(o[:, :], sqr[:, :, :], AX.X, ALU.add).then_inc(ln["var"], 1)
                dve.wait_ge(ln["var"], v)
                dve.tensor_scalar(o[:, :], o[:, :], 1.0 / F, EPS_LN, ALU.mult, ALU.add).then_inc(ln["vareps"], 1)

            def ln_out(ln, v, xo, r, dst):
                dve.wait_ge(ln["rstd"], v)
                dve.scalar_tensor_tensor(out=dst, in0=xo[:, :, :], scalar=0.0, in1=bc(r[:, :], F),
                                         op0=ALU.max, op1=ALU.mult).then_inc(ln["h"], 1)

            def lnA1(T, k, p):
                dve.wait_ge(adj_in[p], 32 * (k + 1))
                ln_centre(lnA, 2 * T + 1, x_t[p], ln_sum, xc)

            def cheb_d1(T, k, p):
                dve.wait_ge(g1_pe, T + 1)
                dve.wait_ge(g3_done, T + 1)
                dve.tensor_tensor(d1[:, :, :].rearrange("n g f -> n (g f)"), ps_a[:, 0:256],
                                  b3x2[:, :, :].rearrange("n g f -> n (g f)"), ALU.subtract).then_inc(g1_done, 1)

            def cheb_x1(T, k, p):
                dve.wait_ge(g0_pe, T + 1)
                dve.tensor_tensor(x1[:, :, :].rearrange("n g f -> n (g f)"), ps_a[:, 0:256],
                                  x_t[p][:, :, :].rearrange("n g f -> n (g f)"), ALU.add).then_inc(x1_done, 1)
                dve.wait_ge(x1_done, T + 1)
                ln_centre(lnA, 2 * T + 2, x1, ln_sum, xc)

            def degrees(T, k, p):
                dve.wait_ge(rs_done, T + 1)
                dve.tensor_scalar(rsp[:, :], ps_a[:, 0:G], 1.0, 1e-30, ALU.add, ALU.max).then_inc(rsp_done, 1)
                dve.tensor_scalar(rsm[:, :], ps_a[:, 0:G], 1.0, 0.0, ALU.add, ALU.is_gt).then_inc(rsp_done, 1)

            def degree_inv(T, k, p):
                dve.wait_ge(dpow_done, T + 1)
                dve.tensor_tensor(dinv[:, :], dinv0[:, :], rsm[:, :], ALU.mult).then_inc(dinv_done, 1)

            def gcn_y(T, k, p):
                dve.wait_ge(hw_pe, T + 1)
                dve.wait_ge(dinv_done, T + 1)
                dve.tensor_tensor(ysc[:, :, :], ps_a[:, 0:256].rearrange("n (g f) -> n g f", g=G), bc(dinv[:, :], F),
                                  ALU.mult).then_inc(y_done, 1)

            def gcn_x2(T, k, p):
                dve.wait_ge(gcn_pe, T + 1)
                dve.scalar_tensor_tensor(out=gcn[:, :, :], in0=ps_a[:, 0:256].rearrange("n (g f) -> n g f", g=G), scalar=0.0,
                                         in1=bc(dinv[:, :], F), op0=ALU.max, op1=ALU.mult).then_inc(gcn_done, 1)
                dve.wait_ge(gcn_done, T + 1)
                dve.tensor_tensor(x2[p][:, :, :], x1[:, :, :], gcn[:, :, :], ALU.add).then_inc(x2_done, 1)

            def lnB1(T, k, p):
                dve.wait_ge(x2_done, T + 1)
                ln_centre(lnB, 2 * T + 1, x2[p], ln2_sum, xc2)

            def norms(T, k, p):
                dve.wait_ge(nsq_done, T + 1)
                dve.tensor_reduce(n2[:, :], sq2[:, :, :], AX.X, ALU.add).then_inc(n2_done, 1)

            def norm_rows(T, k, p):
                dve.wait_ge(nT_done, T + 1)
                dve.tensor_tensor(nTm[:, :, :], nT[:, :].unsqueeze(1).broadcast_to([G, G, 128]),
                                  c32s[0:G, C_NMASK:C_NMASK + 512].rearrange("b (g m) -> b g m", g=G), ALU.mult)\
                    .then_inc(nTm_done, 1)

            def cosines(T, k, p):
                dve.wait_ge(dots_pe, T + 1)
                dve.wait_ge(rD_done, T + 1)
                dve.tensor_tensor(cosm[:, :, :].rearrange("n g m -> n (g m)"), ps_b[:, :], rD[:, :], ALU.mult)\
                    .then_inc(cos_done, 1)

            def logits(T, k, p):
                dve.wait_ge(cos_done, T + 1)
                dve.wait_ge(adj10_done, T + 1)
                dve.scalar_tensor_tensor(out=logit[:, :, :], in0=cosm[:, :, :], scalar=betac[:, 0:1], in1=adj10[p][:, :, :],
                                         op0=ALU.mult, op1=ALU.add).then_inc(logit_done, 1)

            def row_max(T, k, p):
                dve.wait_ge(logit_done, T + 1)
                dve.tensor_reduce(rmax[:, :], logit[:, :, :], AX.X, ALU.max).then_inc(rmax_done, 1)

            def shift(T, k, p):
                dve.wait_ge(rmax_done, T + 1)
                upto(dve, pexp_done, T)
                dve.tensor_tensor(lsh[:, :, :], logit[:, :, :], bc(rmax[:, :], N), ALU.subtract).then_inc(lsh_done, 1)

            def attend(T, k, p):
                o = ps_b[:, 0:G * F].rearrange("n (g f) -> n g f", g=G)
                dve.wait_ge(att_pe, T + 1)
                dve.reciprocal(rsum[:, :], ps_b[:, G * F:G * F + G]).then_inc(rsum_done, 1)
                dve.wait_ge(rsum_done, T + 1)
                dve.tensor_tensor(att[:, :, :], o, bc(rsum[:, :], F), ALU.mult).then_inc(att_done, 1)
                dve.wait_ge(att_done, T + 1)
                upto(dve, stash_out, 32 * T)
                dve.tensor_tensor(x3[p][:, :, :], x2[p][:, :, :], att[:, :, :], ALU.add).then_inc(x3_done, 1)
                dve.wait_ge(x3_done, T + 1)
                ln_centre(lnB, 2 * T + 2, x3[p], ln2_sum, xc2)

            def tree(t, u, q, prods, i):
                w = wbuf[q][:, :].rearrange("k (n s) -> k n s", s=4)
                a = t1[:, :, :]
                b = t2[:, :, :]
                g = 9 * t + u
                if i == 0:
                    dve.wait_ge(w_done, g + 1)
                    dve.tensor_scalar(a, w[:, :, 2:4], 1.0, None, ALU.add).then_inc(t1_done, 1)
                elif i == 1:
                    dve.wait_ge(t1_done, g + 1)
                    dve.scalar_tensor_tensor(out=b, in0=w[:, :, 0:2], scalar=1.0, in1=a, op0=ALU.add, op1=ALU.mult)\
                        .then_inc(t2_done, 1)
                else:
                    dve.wait_ge(t2_done, g + 1)
                    if u == 0:
                        upto(dve, lq_done, LQ_PARTS * (t - 1))
                    if u < UNITS - 1:
                        o, n = prods[:, u % 2, 256 * (u // 2):256 * (u // 2) + 256], b
                        dve.tensor_tensor(o, n[:, :, 0], n[:, :, 1], ALU.mult).then_inc(prod_done, 1)
                    else:
                        o, n = prods[:, :, QH - 128:QH], b.rearrange("k (h n) s -> k h n s", h=2)
                        dve.tensor_tensor(o, n[:, :, :, 0], n[:, :, :, 1], ALU.mult).then_inc(prod_done, 1)

            def sum_slots(T, k, p):
                dve.wait_ge(lq_done, LQ_PARTS * (T + 1))
                upto(dve, sT_pe, T)
                s0, s, r = BLOCKS[0]
                dve.tensor_reduce(sT[:, :, :], lq[p][:, :, 0:r * s // 4].rearrange("k h (r j) -> k h r j", j=s // 4),
                                  AX.X, ALU.add).then_inc(sred_done, 1)

            def combine(T, k, p):
                dve.wait_ge(sperm_pe, T + 1)
                dve.tensor_tensor(osum[:, :, :].rearrange("n g f -> n (g f)"), ps_rank[:, 0:256],
                                  h4[p][:, :, :].rearrange("n g f -> n (g f)"), ALU.mult).then_inc(osum_done, 1)
                dve.wait_ge(osum_done, T + 1)
                upto(dve, out_out[p], 16 * k)
                dve.tensor_tensor(ofin[p][:, :, :], osum[:, :, :], x3[p][:, :, :], ALU.add).then_inc(ofin_done, 1)

            t0 = of(0, 0)
            for r in range(TOP // 8):
                sort_round(*t0, r)
            counts(*t0)
            lnA1(*t0)
            split_parts(*t0)
            check_sorted(*t0)
            ln_var(lnA, 1, sq, var)
            ln_out(lnA, 1, xc, rstd, hcur[:, :, :])
            cheb_d1(*t0)
            cheb_x1(*t0)
            degrees(*t0)
            ln_var(lnA, 2, sq, var)
            ranks(*t0)
            perms(*t0)
            degree_inv(*t0)
            ln_out(lnA, 2, xc, rstd, hcur[:, :, :])
            for r in range(TOP // 8):
                sort_round(*of(0, 1), r)
            check_ranked(*t0)
            gcn_y(*t0)
            gcn_x2(*t0)

            def period(k, p, nxt, nxt2):
                t, k0, p0 = of(k, p)
                n = of(k, p, 1)
                m = of(k, p, 2)
                c = of(k, p)
                b = of(k, p, -1)
                first = isinstance(k, int) and k == 0 and p == 0
                def steps(slot):
                    def at(name, f, *a):
                        if DVE_AT[name] == slot:
                            f(*a)

                    if nxt:
                        at("counts", counts, *n)
                        at("lnA1", lnA1, *n)
                        at("split_parts", split_parts, *n)
                        at("check_sorted", check_sorted, *n)
                        at("ln_var_A1", ln_var, lnA, 2 * t + 3, sq, var)
                        at("ranks", ranks, *n)
                        at("perms", perms, *n)
                        at("ln_out_A1", ln_out, lnA, 2 * t + 3, xc, rstd, hcur[:, :, :])
                        at("check_ranked", check_ranked, *n)
                        at("cheb_d1", cheb_d1, *n)
                        at("cheb_x1", cheb_x1, *n)
                        at("degrees", degrees, *n)
                        at("ln_var_A2", ln_var, lnA, 2 * t + 4, sq, var)
                        at("degree_inv", degree_inv, *n)
                        at("ln_out_A2", ln_out, lnA, 2 * t + 4, xc, rstd, hcur[:, :, :])
                        at("gcn_y", gcn_y, *n)
                        at("gcn_x2", gcn_x2, *n)
                    if nxt2:
                        for r in range(TOP // 8):
                            at(f"max{r}", sort_max, *m, r)
                            if r < TOP // 8 - 1:
                                at(f"remove{r}", sort_remove, *m, r)
                    if not first:
                        at("sum_slots", sum_slots, *b)
                        at("combine", combine, *b)
                    at("lnB1", lnB1, *c)
                    at("ln_var_B1", ln_var, lnB, 2 * t + 1, sq2, var2)
                    at("ln_out_B1", ln_out, lnB, 2 * t + 1, xc2, rstd2, h2[:, :, :])
                    at("norms", norms, *c)
                    at("norm_rows", norm_rows, *c)
                    at("cosines", cosines, *c)
                    at("logits", logits, *c)
                    at("row_max", row_max, *c)
                    at("shift", shift, *c)
                    at("attend", attend, *c)
                    at("ln_var_B2", ln_var, lnB, 2 * t + 2, sq2, var2)
                    at("ln_out_B2", ln_out, lnB, 2 * t + 2, xc2, rstd2, h4[p][:, :, :])

                for u in range(UNITS):
                    tu = (t if u else t - 1, (u - 1) % UNITS, (p + u - 1) % 2, prod[p] if u else prod[1 - p])
                    steps(4 * u)
                    steps(4 * u + 1)
                    if not (first and u == 0):
                        tree(*tu, 0)
                    steps(4 * u + 2)
                    if not (first and u == 0):
                        tree(*tu, 1)
                        tree(*tu, 2)
                    steps(4 * u + 3)

            periods(dve, period)
            for i in range(3):
                tree(NT - 1, UNITS - 1, (1 + UNITS - 1) % 2, prod[1], i)
            sum_slots(*of(NT // 2 - 1, 1))
            combine(*of(NT // 2 - 1, 1))
            dve.wait_ge(flag_pe, 1)
            dve.tensor_reduce(flagf[:, :], ps_a[0:1, 0:128], AX.X, ALU.max).then_inc(flag_dve, 1)
            dve.wait_ge(flag_dve, 1)
            dve.tensor_scalar(flagi[:, :], flagf[:, :], 0.0, None, ALU.is_gt).then_inc(flag_dve, 1)

            def body(dve):
                dve.memset(gones, 1.0)
                dve.memset(gh[F:128, :], 0.0)
                dve.memset(gsum[F:128, :, :], 0.0).then_inc(gones_done, 1)
                def round_(it):
                    for s in range(STEPS):
                        n = STEPS * it + s
                        dve.wait_ge(gsp_done, 2 * n + 1)
                        dve.tensor_tensor(gh[0:F, :], grel, glog, ALU.add).then_inc(gh_done, 1)
                        dve.wait_ge(gsp_done, 2 * n + 2)
                        dve.tensor_tensor(gw, grel, glog, ALU.add).then_inc(gw_done, 1)
                        dve.wait_ge(gw_done, n + 1)
                        dve.tensor_reduce(gsum[0:F, :, :].rearrange("f a b -> f (a b)"), gw.rearrange("f (i j) -> f i j", j=N), AX.X, ALU.add)\
                            .then_inc(gred_done, 1)
                        dve.wait_ge(gred_done, n + 1)
                        dve.tensor_scalar(gsum[0:F, :, :], gsum[0:F, :, :], -N * LOG2, None, ALU.add).then_inc(gsum_done, 1)

                loop(dve, ROUNDS, round_)
                def finish(T):
                    dve.wait_ge(gx_in, 48 * T + 48)
                    dve.tensor_tensor(gS[:, :, :], gS[:, :, :], gx[1][:, :, :], ALU.mult).then_inc(gmul_done, 1)
                    dve.wait_ge(gmul_done, T + 1)
                    upto(dve, gout_out, 16 * T)
                    dve.tensor_tensor(ofin[0][:, :, :], gS[:, :, :], gx[0][:, :, :], ALU.add).then_inc(gfin_done, 1)

                loop(dve, NT, finish)

            general(dve, body)


_INS = ["x", "adj", "L0_gnn_theta", "L1_gnn_kernel", "L2_gnn_beta", "L3_gnn_W1", "L3_gnn_b1", "L3_gnn_W2", "L3_gnn_b2"]


def kernel(**inputs):
    import numpy as _np
    import concourse.bacc as _bacc
    from concourse import mybir as _mybir
    from concourse.bass_utils import run_bass_kernel_spmd as _run

    nc = _bacc.Bacc("TRN2", target_bir_lowering=False, num_devices=1)
    arrays, args = {}, []
    c32, c16 = tables()
    for name, a in [(n, _np.ascontiguousarray(inputs[n])) for n in _INS] + [("table32", c32), ("table16", c16)]:
        arrays[f"in_{name}"] = a
        args.append(nc.dram_tensor(f"in_{name}", a.shape, _mybir.dt.from_np(a.dtype), kind="ExternalInput").ap())
    out = nc.dram_tensor("out_0", inputs["x"].shape, _mybir.dt.float32, kind="ExternalOutput").ap()
    adjacency_layers(nc, *args, out)
    return _run(nc, [arrays], core_ids=[0]).results[0]["out_0"]
```

```python
import concourse.bass as bass
from concourse import mybir
from contextlib import ExitStack

F32 = mybir.dt.float32
F16 = mybir.dt.float16
I32 = mybir.dt.int32
ALU = mybir.AluOpType
ACT = mybir.ActivationFunctionType
AX = mybir.AxisListType

N = 128
F = 64
G = 4
KF = 32
KALL = 150
DMAX = 0.2
GAMMA = 10.0
LOG2 = 0.6931471805599453
EPS_LN = 1e-5
EPS_COS = 1e-7
TOP = 56
BLOCKS = [(0, 28, 128), (28, 4, 112), (32, 4, 80), (36, 4, 32), (40, 4, 16), (44, 4, 8), (48, 8, 4)]
COLS = sum(s * r for _, s, r in BLOCKS)
UNITS = COLS // 512
QH = COLS // 4
LQ_PARTS = 3
QP = QH // LQ_PARTS
NPART = 4
PW = NPART * (TOP + 1)
ONES = 32
DSCALE = 256.0
QSCALE = 1024.0
C_ID, C_MISS, C_NMASK, C_BIAS, C_EMAX, C_CAP, C_NLOG, C_CEN = 0, 128, 256, 768, 769, 770, 771, 772
NC32 = 774
H_ID, H_P128, H_N128, H_CMAT, H_IOTA, H_ARGW = 0, 128, 256, 384, 512, 640
NC16 = 768

PE_AT = {"adjT": 1, "delta": 5, "hT0": 6, "rank_parts0": 7, "cheb3": 7, "rank_parts1": 9, "cheb2": 9, "cheb1": 10,
    "h2T_mm": 11, "nT_mm": 14, "cheb0": 15, "sT_mm": 16, "D_mm": 16, "row_sums": 17, "sperm": 17, "dots": 18,
    "hT1": 21, "pT_mm": 24, "att_mm": 29, "hw": 30, "permT": 32, "gcn_mm": 32}
ACT_AT = {"copy_adjT": 4, "copy_hT0": 8, "copy_ranked0": 8, "twice_b3": 9, "log22": 11, "twice_b2": 11,
    "copy_ranked1": 15, "copy_h2T": 15, "copy_nT": 17, "copy_sR": 19, "log_D": 19, "recip_D": 19, "log20": 23,
    "exp_logits": 24, "copy_hT1": 28, "copy_pT": 29, "log21": 31, "copy_permT": 35}
DVE_AT = {"lnA1": 0, "counts": 1, "split_parts": 3, "check_sorted": 3, "ln_var_A1": 4, "ln_out_A1": 4, "lnB1": 5,
    "ranks": 5, "perms": 5, "max0": 6, "ln_var_B1": 8, "ln_out_B1": 8, "negatives": 9, "norms": 11, "sum_slots": 12,
    "cheb_d1": 14, "check_ranked": 15, "remove0": 15, "max1": 16, "norm_rows": 16, "cheb_x1": 17, "remove1": 17,
    "degrees": 19, "ln_var_A2": 19, "max2": 19, "remove2": 19, "degree_inv": 20, "cosines": 20, "ln_out_A2": 20,
    "logits": 20, "row_max": 20, "shift": 20, "max3": 22, "remove3": 22, "max4": 23, "remove4": 25, "max5": 26,
    "combine": 27, "remove5": 29, "max6": 30, "gcn_y": 31, "attend": 31, "ln_var_B2": 31, "gcn_x2": 32,
    "ln_out_B2": 34}
POOL_AT = {"ln_square_A1": 1, "count_diag": 2, "ln_power_A1": 2, "ln_square_B1": 5, "ln_power_B1": 8,
    "norm_square": 8, "beside_ones": 8, "norm_power": 11, "close_sums": 12, "ln_square_A2": 14, "degree_power": 17,
    "ln_power_A2": 17, "adj_times_10": 19, "ln_square_B2": 27, "ln_power_B2": 29}


def tables():
    import numpy as np
    c = np.zeros((128, NC32), np.float32)
    h = np.zeros((128, NC16), np.float16)
    slots = np.zeros(128)
    for _, s, r in BLOCKS:
        slots[:r] += s
    c[:, C_ID:C_ID + 128] = np.eye(128)
    c[:, C_MISS:C_MISS + 128] = N - slots[None, :]
    for g in range(G):
        c[g, C_NMASK + 128 * g:C_NMASK + 128 * g + 128] = 1.0
    k = np.arange(128) % KF
    cen = (np.float32(0.1) * np.arange(KALL, dtype=np.float32)).astype(np.float64)
    c[:, C_BIAS] = -GAMMA * cen[k] ** 2
    c[:, C_EMAX] = np.exp(-GAMMA * np.maximum(cen[k] - DMAX, 0) ** 2) * 1.0001
    c[:, C_CAP] = slots
    c[:, C_NLOG] = -LOG2
    c[:, C_CEN] = -cen[:128]
    c[:KALL - 128, C_CEN + 1] = -cen[128:]
    i = np.arange(128)
    h[:, H_ID:H_ID + 128] = np.eye(128)
    h[:, H_P128:H_P128 + 128] = 128.0
    h[:, H_N128:H_N128 + 128] = -128.0
    h[:, H_CMAT:H_CMAT + 128] = i[:, None] - i[None, :]
    h[:, H_IOTA:H_IOTA + 128] = i[None, :]
    for g in range(G):
        for q, w in enumerate((2 * GAMMA * 0.1 / DSCALE, 2 * GAMMA * 0.1 / DSCALE, -GAMMA / QSCALE, -GAMMA / QSCALE)):
            h[NPART * g + q, H_ARGW + KF * g:H_ARGW + KF * (g + 1)] = w * (np.arange(KF) if q < 2 else 1.0)
    rest = -GAMMA * cen[k] ** 2
    for q in range(3):
        h[ONES + q, H_ARGW:H_ARGW + 128] = rest
        rest = rest - h[ONES + q, H_ARGW:H_ARGW + 128].astype(np.float64)
    return c, h


def adjacency_layers(nc, x, adj, theta, wk, beta, w1, b1, w2, b2, c32, c16, out):
    B = x.shape[0]
    NT = B // G
    assert B % (2 * G) == 0 and NT >= 8 and UNITS == 9
    rows_dram = [nc.dram_tensor(f"arg_rows{p}", [NPART * G, COLS], F16, kind="Internal").ap() for p in range(2)]
    s_dram = nc.dram_tensor("s_rows", [B * 8, 4, 4, F], F32, kind="Internal").ap()
    scratch = nc.dram_tensor("x3_h4", [NT, 128, 2, G * F], F32, kind="Internal").ap()

    with ExitStack() as ctx:
        def sb(name, shape, dt=F32):
            return ctx.enter_context(nc.sbuf_tensor(name, shape, dt))

        def sem(name):
            return ctx.enter_context(nc.semaphore(name))

        c32s = sb("c32s", [128, NC32])
        c16s = sb("c16s", [128, NC16], F16)
        w1z = sb("w1z", [128, 2, 128])
        w2bd = sb("w2bd", [128, 128])
        b1c = sb("b1c", [128, 1])
        b2c = sb("b2c", [128, 1])
        b2p = sb("b2p", [128, 1])
        einv = sb("einv", [128, 1])
        thin = sb("thin", [128, 4, F])
        th = sb("th", [128, 4, 128])
        wks = sb("wks", [128, 128])
        betac = sb("betac", [128, 1])
        onesc = sb("onesc", [128, 1])
        kmat = sb("kmat", [128, 2, 128])
        setup = sb("setup", [128, 16])
        wpos1, wneg1, wpos2, wneg2 = (sb(n, [128, 128]) for n in ("wpos1", "wneg1", "wpos2", "wneg2"))
        epsc = sb("epsc", [128, 1])
        bad = sb("bad", [128, 1])
        badneg = sb("badneg", [128, 1])
        flagf = sb("flagf", [1, 1])
        flagi = sb("flagi", [1, 1], I32)

        adj_t = [sb(f"adj_t{p}", [128, G, N]) for p in range(2)]
        x_t = [sb(f"x_t{p}", [128, G, F]) for p in range(2)]
        srt_w = sb("srt_w", [128, G, N])
        gate = sb("gate", [128, 1])
        srt = sb("srt", [128, G, TOP])
        nz = sb("nz", [128, G, TOP])
        cnt = sb("cnt", [128, G])
        srt_c = sb("srt_c", [128, G, TOP])
        dsq = sb("dsq", [128, G, TOP])
        parts = sb("parts", [128, G, NPART, TOP + 1], F16)
        diag = sb("diag", [128, G, 128], F16)
        rank = sb("rank", [128, G])
        junk = sb("junk", [128, G, 128], F16)
        junkn = sb("junkn", [128, G * N], F16)
        junk4 = sb("junk4", [128, 4])
        perm = sb("perm", [128, G, 128], F16)
        perm_t = [sb(f"perm_t{p}", [128, G, 128]) for p in range(2)]
        parts_r = sb("parts_r", [128, G, NPART, TOP + 1], F16)
        argin = [sb(f"argin{p}", [128, COLS], F16) for p in range(2)]

        adj_tr = sb("adj_tr", [128, G, N])
        adj10 = [sb(f"adj10_{p}", [128, G, N]) for p in range(2)]
        ln_sum = sb("ln_sum", [128, G])
        xc = sb("xc", [128, G, F])
        sq = sb("sq", [128, G, F])
        var = sb("var", [128, G])
        rstd = sb("rstd", [128, G])
        expo = sb("expo", [128, G])
        ten = sb("ten", [128, 1])
        half = sb("half", [128, G])
        ln2_sum = sb("ln2_sum", [128, G])
        xc2 = sb("xc2", [128, G, F])
        sq2 = sb("sq2", [128, G, F])
        var2 = sb("var2", [128, G])
        rstd2 = sb("rstd2", [128, G])
        hcur = sb("hcur", [128, G, F])
        hT = sb("hT", [128, 2, 128])
        b3x2 = sb("b3x2", [128, G, F])
        b2x2 = sb("b2x2", [128, G, F])
        d1 = sb("d1", [128, G, F])
        x1 = sb("x1", [128, G, F])
        rsp = sb("rsp", [128, G])
        rsm = sb("rsm", [128, G])
        dinv0 = sb("dinv0", [128, G])
        dinv = sb("dinv", [128, G])
        ysc = sb("ysc", [128, G, F])
        gcn = sb("gcn", [128, G, F])
        x2 = [sb(f"x2_{p}", [128, G, F]) for p in range(2)]
        h2 = sb("h2", [128, G, F])
        h2o = sb("h2o", [128, G, F + 1])
        h2T = sb("h2T", [128, G, 128])
        n2 = sb("n2", [128, G])
        nrm = sb("nrm", [128, G])
        nT = sb("nT", [G, 128])
        nTm = sb("nTm", [G, G, 128])
        lnD = sb("lnD", [128, G * N])
        rD = sb("rD", [128, G * N])
        cosm = sb("cosm", [128, G, N])
        logit = sb("logit", [128, G, N])
        rmax = sb("rmax", [128, G])
        lsh = sb("lsh", [128, G, N])
        pexp = sb("pexp", [128, G, N])
        pT = sb("pT", [128, G, N])
        rsum = sb("rsum", [128, G])
        att = sb("att", [128, G, F])
        x3 = [sb(f"x3_{p}", [128, G, F]) for p in range(2)]
        h4 = [sb(f"h4_{p}", [128, G, F]) for p in range(2)]

        ebuf = [sb(f"ebuf{i}", [128, 1024]) for i in range(2)]
        sbuf1 = [sb(f"sbuf1_{i}", [128, 1024]) for i in range(2)]
        hbuf = [sb(f"hbuf{i}", [128, 1024]) for i in range(2)]
        wbuf = [sb(f"wbuf{i}", [128, 1024]) for i in range(2)]
        t1 = [sb(f"t1_{i}", [128, 256, 2]) for i in range(2)]
        t2 = [sb(f"t2_{i}", [128, 256, 2]) for i in range(2)]
        prod = [sb(f"prod{p}", [128, 2, QH]) for p in range(2)]
        lq = [sb(f"lq{p}", [128, 2, QH]) for p in range(2)]
        sT = sb("sT", [128, 2, 128])
        sR = sb("sR", [128, G, F])
        osum = sb("osum", [128, G, F])
        ofin = [sb(f"ofin{p}", [128, G, F]) for p in range(2)]

        ps_arg = ctx.enter_context(nc.psum_tensor("ps_arg", [128, 512], F32))
        ps_v1 = ctx.enter_context(nc.psum_tensor("ps_v1", [128, 1024], F32))
        ps_v2 = ctx.enter_context(nc.psum_tensor("ps_v2", [128, 1024], F32))
        ps_rank = ctx.enter_context(nc.psum_tensor("ps_rank", [128, 512], F32))
        ps_a = ctx.enter_context(nc.psum_tensor("ps_a", [128, 512], F32))
        ps_b = ctx.enter_context(nc.psum_tensor("ps_b", [128, 512], F32))
        ps_rank16 = ps_rank[:, 0:256].bitcast(F16)

        tables_in, consts_in, wz_done = sem("tables_in"), sem("consts_in"), sem("wz_done")
        setup_pe, setup_act, setup_dve = sem("setup_pe"), sem("setup_act"), sem("setup_dve")
        setup_pool = sem("setup_pool")
        adj_in = [sem("adj_in0"), sem("adj_in1")]
        sort_step = sem("sort_step")
        cnt_done, parts_done, diag_done, delta_done, rank_done, perm_done = (
            sem("cnt_done"), sem("parts_done"), sem("diag_done"), sem("delta_done"), sem("rank_done"), sem("perm_done"))
        rows_out = sem("rows_out")
        permT_pe, permT_done, pr_pe, pr_done, rows_in, check_step, neg_done = (
            sem("permT_pe"), sem("permT_done"), sem("pr_pe"), sem("pr_done"), sem("rows_in"), sem("check_step"), sem("neg_done"))
        nz_done, srtc_done, part_step = sem("nz_done"), sem("srtc_done"), sem("part_step")
        arg_done, e_done, v1_done, s1_done, h_done, v2_done, w_done = (
            sem("arg_done"), sem("e_done"), sem("v1_done"), sem("s1_done"), sem("h_done"), sem("v2_done"), sem("w_done"))
        t1_done, t2_done, prod_done, lq_done = sem("t1_done"), sem("t2_done"), sem("prod_done"), sem("lq_done")
        adjT_pe, adjT_done, adj10_done = sem("adjT_pe"), sem("adjT_done"), sem("adj10_done")
        lnA = {k: sem(f"lnA_{k}") for k in ("sum", "xc", "sq", "var", "vareps", "rstd", "h")}
        lnB = {k: sem(f"lnB_{k}") for k in ("sum", "xc", "sq", "var", "vareps", "rstd", "h")}
        hT_pe, hT_done = sem("hT_pe"), sem("hT_done")
        g3_pe, g3_done, g2_pe, g2_done, g1_pe, g1_done, g0_pe, x1_done = (
            sem("g3_pe"), sem("g3_done"), sem("g2_pe"), sem("g2_done"), sem("g1_pe"), sem("g1_done"), sem("g0_pe"), sem("x1_done"))
        rs_done, rsp_done, dpow_done, dinv_done = sem("rs_done"), sem("rsp_done"), sem("dpow_done"), sem("dinv_done")
        hw_pe, y_done, gcn_pe, gcn_done, x2_done = sem("hw_pe"), sem("y_done"), sem("gcn_pe"), sem("gcn_done"), sem("x2_done")
        h2T_pe, h2T_done, h2o_done, nsq_done, n2_done, nrm_done = (
            sem("h2T_pe"), sem("h2T_done"), sem("h2o_done"), sem("nsq_done"), sem("n2_done"), sem("nrm_done"))
        nT_pe, nT_done, nTm_done, D_pe, lnD_done, rD_done = (
            sem("nT_pe"), sem("nT_done"), sem("nTm_done"), sem("D_pe"), sem("lnD_done"), sem("rD_done"))
        dots_pe, cos_done, logit_done, rmax_done, lsh_done, pexp_done = (
            sem("dots_pe"), sem("cos_done"), sem("logit_done"), sem("rmax_done"), sem("lsh_done"), sem("pexp_done"))
        pT_pe, pT_done, att_pe, rsum_done, att_done, x3_done = (
            sem("pT_pe"), sem("pT_done"), sem("att_pe"), sem("rsum_done"), sem("att_done"), sem("x3_done"))
        stash_out = sem("stash_out")
        sred_done, stail_step, sT_pe, sR_done, sperm_pe, osum_done, ofin_done = (
            sem("sred_done"), sem("stail_step"), sem("sT_pe"), sem("sR_done"), sem("sperm_pe"), sem("osum_done"), sem("ofin_done"))
        gw_in, gones_done, gd_in, gbc_pe, gsq_done, ge_done, gv1_pe, gv2_pe = (
            sem("gw_in"), sem("gones_done"), sem("gd_in"), sem("gbc_pe"), sem("gsq_done"), sem("ge_done"), sem("gv1_pe"), sem("gv2_pe"))
        gabs_done, gexp_done, gsp_done, gh_done, gw_done, gred_done, gsum_done, gT_pe, grow_done, grow_out = (
            sem("gabs_done"), sem("gexp_done"), sem("gsp_done"), sem("gh_done"), sem("gw_done"), sem("gred_done"), sem("gsum_done"),
            sem("gT_pe"), sem("grow_done"), sem("grow_out"))
        gx_in, gmul_done, gfin_done, gout_out = sem("gx_in"), sem("gmul_done"), sem("gfin_done"), sem("gout_out")
        out_out = [sem("out_out0"), sem("out_out1")]
        flag_pe, flag_dve = sem("flag_pe"), sem("flag_dve")
        TAIL = 1 + sum(s // 4 for _, s, _ in BLOCKS[1:])

        def upto(e, s, v):
            if isinstance(v, int) and v <= 0:
                return
            e.wait_ge(s, v)

        ident = c32s[:, C_ID:C_ID + 128]
        id16 = c16s[:, H_ID:H_ID + 128]

        def ebuf_of(p, c):
            return ebuf[(p + c) % 2]

        def bc(col, n):
            return col.unsqueeze(2).broadcast_to([128, G, n])

        SLOTS = 4 * UNITS
        CHECKS = 3
        SORT_STEPS = 2 * (TOP // 8) - 1
        ROWS_DMA = 16 * len(BLOCKS)
        N_CONST = 16 * (G + 10 + 1)

        offs, at = [], 0
        for s0, s, r in BLOCKS:
            offs.append(at)
            at += s * r

        def of(k, p, d=0):
            q = p + d
            return 2 * k + q, k + q // 2, q % 2

        def tile_slice(T):
            return slice(T * G, T * G + G) if isinstance(T, int) else bass.ds(T * G, G)

        def periods(e, period):
            for k in range(2):
                period(k, 0, True, True)
                period(k, 1, True, True)
            with e.Fori(2, NT // 2 - 1) as k:
                period(k, 0, True, True)
                period(k, 1, True, True)
            period(NT // 2 - 1, 0, True, False)
            period(NT // 2 - 1, 1, False, False)

        ROUNDS, STEPS, W = B * 8, 4, 512
        gd = ebuf[0][0:1, :], ebuf[1][0:1, :]
        gsq = hbuf[0]
        ge = hbuf[1]
        gw1 = sbuf1[0][:, 0:F], sbuf1[0][0:KALL - 128, F:2 * F]
        gones = sbuf1[0][0:1, 128:256]
        gabs, grel = sbuf1[1][0:F, 0:W], sbuf1[1][0:F, W:2 * W]
        gexp, glog = wbuf[0][0:F, 0:W], wbuf[0][0:F, W:2 * W]
        gh, gw = wbuf[1][:, 0:W], wbuf[1][0:F, W:2 * W]
        gsum = t1[0][:, 0:2, :]
        grow = osum[0:4, :, :]
        gx = [x3[0], h4[0]]
        gS = sR

        def loop(e, count, step):
            step(0)
            with e.Fori(1, count) as i:
                step(i)

        def at_index(i):
            return slice(i, i + 1) if isinstance(i, int) else bass.ds(i, 1)

        def general(e, body):
            e.wait_ge(flag_dve, 2)
            flag = e.value_load(flagi[0:1, 0:1])
            with e.If(flag > 0):
                body(e)

        block = ctx.enter_context(nc.Block())

        @block.sync
        def _(sp):
            def load(T, k, p):
                upto(sp, sort_step, SORT_STEPS * (T - 1))
                upto(sp, adjT_pe, T - 1)
                upto(sp, adj10_done, T - 1)
                upto(sp, neg_done, T - 1)
                upto(sp, x1_done, T - 1)
                sp.dma_start(adj_t[p][:, :, :], adj[tile_slice(T)].rearrange("g i j -> i g j")).then_inc(adj_in[p], 16)
                sp.dma_start(x_t[p][:, :, :], x[tile_slice(T)].rearrange("g i f -> i g f")).then_inc(adj_in[p], 16)

            def spread_rows(T, k, p):
                upto(sp, arg_done, UNITS * (T - 1))
                sp.wait_ge(pr_done, 2 * T + 2)
                for (s0, s, r), o in zip(BLOCKS, offs):
                    src = parts_r[0:r, :, :, :].rearrange("r g q s -> r (g q) s")[:, :, s0:s0 + s]
                    dst = rows_dram[p][:, o:o + s * r].rearrange("q (r s) -> r q s", s=s)
                    sp.dma_start(dst, src).then_inc(rows_out, 16)
                sp.wait_ge(rows_out, ROWS_DMA * (T + 1))
                sp.dma_start(argin[p][0:NPART * G, :], rows_dram[p][:, :]).then_inc(rows_in, 16)

            def store_x3(T, k, p):
                sp.wait_ge(x3_done, T + 1)
                sp.wait_ge(lnB["h"], 2 * T + 2)
                dst = scratch[slice(T, T + 1) if isinstance(T, int) else bass.ds(T, 1)].rearrange("o n a f -> (o n) a f")
                sp.dma_start(dst[:, 0, :], x3[p][:, :, :].rearrange("n g f -> n (g f)")).then_inc(stash_out, 16)
                sp.dma_start(dst[:, 1, :], h4[p][:, :, :].rearrange("n g f -> n (g f)")).then_inc(stash_out, 16)

            def store_out(T, k, p):
                sp.wait_ge(ofin_done, T + 1)
                sp.dma_start(out[tile_slice(T)].rearrange("g n f -> n g f"), ofin[p][:, :, :]).then_inc(out_out[p], 16)

            load(*of(0, 0))
            sp.dma_start(c16s[:, :], c16[:, :]).then_inc(tables_in, 16)
            sp.dma_start(c32s[:, :], c32[:, :]).then_inc(tables_in, 16)
            sp.wait_ge(wz_done, 1)
            for g in range(G):
                sp.dma_start(w1z[KF * g:KF * g + KF, g // 2, F * (g % 2):F * (g % 2) + F], w1[0:KF, :]).then_inc(consts_in, 16)
            for g in range(2):
                r = slice(F * g, F * g + F)
                sp.dma_start(w2bd[r, r], w2[:, :]).then_inc(consts_in, 16)
                sp.dma_start(b1c[r, :], b1.rearrange("(f o) -> f o", o=1)).then_inc(consts_in, 16)
                sp.dma_start(b2c[r, :], b2.rearrange("(f o) -> f o", o=1)).then_inc(consts_in, 16)
                sp.dma_start(wks[r, r], wk[:, :]).then_inc(consts_in, 16)
                sp.dma_start(thin[r, :, :], theta.rearrange("k c f -> c k f")).then_inc(consts_in, 16)
            sp.dma_start(betac[:, :], beta.rearrange("(o b) -> o b", o=1).broadcast_to([128, 1])).then_inc(consts_in, 16)
            load(*of(0, 1))
            sp.wait_ge(wz_done, 10)
            spread_rows(*of(0, 0))

            def period(k, p, nxt, nxt2):
                if nxt2:
                    load(*of(k, p, 2))
                if nxt:
                    spread_rows(*of(k, p, 1))
                if not (isinstance(k, int) and k == 0 and p == 0):
                    store_out(*of(k, p, -1))
                store_x3(*of(k, p))

            periods(sp, period)
            store_out(*of(NT // 2 - 1, 1))
            sp.wait_ge(stash_out, 32 * NT)
            for p in range(2):
                sp.wait_ge(out_out[p], 16 * (NT // 2))

            def body(sp):
                sp.dma_start(gw1[0], w1[0:128, :]).then_inc(gw_in, 16)
                sp.dma_start(gw1[1], w1[128:KALL, :]).then_inc(gw_in, 16)
                adj_rounds = adj.rearrange("b (r s) j -> (b r) (s j)", s=16)
                def round_(it):
                    upto(sp, gbc_pe, STEPS * it)
                    src = adj_rounds[at_index(it)]
                    for i in range(2):
                        sp.dma_start(gd[i], src[:, 1024 * i:1024 * i + 1024]).then_inc(gd_in, 16)
                    sp.wait_ge(grow_done, STEPS * it + STEPS)
                    sp.dma_start(s_dram[at_index(it)].rearrange("o s q f -> (o q) s f"), grow).then_inc(grow_out, 16)

                loop(sp, ROUNDS, round_)
                sp.wait_ge(grow_out, 16 * ROUNDS)
                def finish(T):
                    upto(sp, gmul_done, T)
                    upto(sp, gfin_done, T)
                    src = scratch[at_index(T)].rearrange("o n a f -> (o n) a f")
                    for a in range(2):
                        sp.dma_start(gx[a][:, :, :].rearrange("n g f -> n (g f)"), src[:, a, :]).then_inc(gx_in, 16)
                    s_rows = s_dram.rearrange("(b r) s q f -> b (r s q) f", r=8)
                    sp.dma_start(gS[:, :, :], s_rows[tile_slice(T)].rearrange("g n f -> n g f")).then_inc(gx_in, 16)
                    sp.wait_ge(gfin_done, T + 1)
                    sp.dma_start(out[tile_slice(T)].rearrange("g n f -> n g f"), ofin[0][:, :, :]).then_inc(gout_out, 16)

                loop(sp, NT, finish)
                sp.wait_ge(gout_out, 16 * NT)

            general(sp, body)

        @block.gpsimd
        def _(pool):
            pool.memset(w1z[:, :, :], 0.0).then_inc(setup_pool, 1)
            pool.memset(w2bd[:, :], 0.0).then_inc(setup_pool, 1)
            pool.memset(wks[:, :], 0.0).then_inc(setup_pool, 1)
            pool.memset(expo[:, :], -0.5).then_inc(setup_pool, 1)
            pool.memset(half[:, :], 0.5).then_inc(setup_pool, 1)
            pool.memset(ten[:, :], 10.0).then_inc(setup_pool, 1)
            pool.wait_ge(setup_pool, 6)
            pool.memset(onesc[:, :], 1.0).then_inc(wz_done, 1)
            pool.memset(th[:, :, :], 0.0).then_inc(wz_done, 1)
            pool.memset(h2T[:, :, :], 0.0).then_inc(wz_done, 1)
            pool.memset(h2o[:, :, F:F + 1], 1.0).then_inc(wz_done, 1)
            pool.memset(parts[:, :, :, TOP:TOP + 1], 0.0).then_inc(wz_done, 1)
            pool.memset(badneg[:, :], 0.0).then_inc(wz_done, 1)
            for p in range(2):
                pool.memset(argin[p][:, :], 0.0).then_inc(wz_done, 1)
            for p in range(2):
                pool.wait_ge(wz_done, 8 + p)
                pool.memset(argin[p][ONES:64, :], 1.0).then_inc(wz_done, 1)

            def ln_square(ln, v, a, o):
                pool.wait_ge(ln["xc"], v)
                pool.tensor_tensor(o[:, :, :], a[:, :, :], a[:, :, :], ALU.mult).then_inc(ln["sq"], 1)

            def ln_power(ln, v, a, o):
                pool.wait_ge(ln["vareps"], v)
                pool.tensor_tensor(o[:, :], a[:, :], expo[:, :], ALU.pow).then_inc(ln["rstd"], 1)

            def count_diag(T, k, p):
                pool.wait_ge(cnt_done, T + 1)
                upto(pool, delta_done, T)
                pool.tensor_tensor(diag[:, :, :], id16.unsqueeze(1).broadcast_to([128, G, 128]), bc(cnt[:, :], 128),
                                   ALU.mult).then_inc(diag_done, 1)

            def adj_times_10(T, k, p):
                pool.wait_ge(adj_in[p], 32 * (k + 1))
                upto(pool, logit_done, T - 1)
                pool.tensor_tensor(adj10[p][:, :, :], adj_t[p][:, :, :], ten[:, :].unsqueeze(2).broadcast_to([128, G, N]), ALU.mult)\
                    .then_inc(adj10_done, 1)

            def degree_power(T, k, p):
                pool.wait_ge(rsp_done, 2 * T + 2)
                pool.tensor_tensor(dinv0[:, :], rsp[:, :], expo[:, :], ALU.pow).then_inc(dpow_done, 1)

            def norm_square(T, k, p):
                pool.wait_ge(lnB["h"], 2 * T + 1)
                pool.tensor_tensor(sq2[:, :, :], h2[:, :, :], h2[:, :, :], ALU.mult).then_inc(nsq_done, 1)

            def beside_ones(T, k, p):
                pool.wait_ge(lnB["h"], 2 * T + 1)
                upto(pool, att_pe, T)
                pool.tensor_tensor(h2o[:, :, 0:F], h2[:, :, :], h2o[:, :, F:F + 1].broadcast_to([128, G, F]), ALU.mult)\
                    .then_inc(h2o_done, 1)

            def norm_power(T, k, p):
                pool.wait_ge(n2_done, T + 1)
                pool.tensor_tensor(nrm[:, :], n2[:, :], half[:, :], ALU.pow).then_inc(nrm_done, 1)

            def product(t, u, q, prods):
                pool.wait_ge(t2_done, UNITS * t + u + 1)
                if u == 0:
                    upto(pool, lq_done, LQ_PARTS * (t - 1))
                n = t2[q][:, :, :]
                if u < UNITS - 1:
                    o = prods[:, u % 2, 256 * (u // 2):256 * (u // 2) + 256]
                    pool.tensor_tensor(o, n[:, :, 0], n[:, :, 1], ALU.mult).then_inc(prod_done, 1)
                else:
                    n = n.rearrange("k (h n) s -> k h n s", h=2)
                    pool.tensor_tensor(prods[:, :, QH - 128:QH], n[:, :, :, 0], n[:, :, :, 1], ALU.mult).then_inc(prod_done, 1)

            def close_sums(T, k, p):
                pool.wait_ge(sred_done, T + 1)
                pool.tensor_tensor(sT[:, :, :], sT[:, :, :], kmat[:, :, :], ALU.add).then_inc(stail_step, 1)
                n = 1
                for (s0, s, r), o in list(zip(BLOCKS, offs))[1:]:
                    for j in range(s // 4):
                        v = lq[p][:, :, o // 4:o // 4 + r * s // 4].rearrange("k h (r j) -> k h r j", j=s // 4)[:, :, :, j]
                        pool.wait_ge(stail_step, TAIL * T + n)
                        pool.tensor_tensor(sT[:, :, 0:r], sT[:, :, 0:r], v, ALU.add).then_inc(stail_step, 1)
                        n += 1
                assert n == TAIL

            pool.wait_ge(wz_done, 10)
            pool.wait_ge(tables_in, 32)
            t0 = of(0, 0)
            count_diag(*t0)
            ln_square(lnA, 1, xc, sq)
            ln_power(lnA, 1, var, rstd)
            adj_times_10(*t0)
            ln_square(lnA, 2, xc, sq)
            degree_power(*t0)
            ln_power(lnA, 2, var, rstd)

            def period(k, p, nxt, nxt2):
                t, k0, p0 = of(k, p)
                n = of(k, p, 1)
                c = of(k, p)
                b = of(k, p, -1)
                first = isinstance(k, int) and k == 0 and p == 0

                def steps(slot):
                    def at(name, f, *a):
                        if POOL_AT[name] == slot:
                            f(*a)

                    if nxt:
                        at("count_diag", count_diag, *n)
                        at("ln_square_A1", ln_square, lnA, 2 * t + 3, xc, sq)
                        at("ln_power_A1", ln_power, lnA, 2 * t + 3, var, rstd)
                        at("adj_times_10", adj_times_10, *n)
                        at("ln_square_A2", ln_square, lnA, 2 * t + 4, xc, sq)
                        at("degree_power", degree_power, *n)
                        at("ln_power_A2", ln_power, lnA, 2 * t + 4, var, rstd)
                    if not first:
                        at("close_sums", close_sums, *b)
                    at("ln_square_B1", ln_square, lnB, 2 * t + 1, xc2, sq2)
                    at("ln_power_B1", ln_power, lnB, 2 * t + 1, var2, rstd2)
                    at("norm_square", norm_square, *c)
                    at("norm_power", norm_power, *c)
                    at("beside_ones", beside_ones, *c)
                    at("ln_square_B2", ln_square, lnB, 2 * t + 2, xc2, sq2)
                    at("ln_power_B2", ln_power, lnB, 2 * t + 2, var2, rstd2)

                for u in range(UNITS):
                    steps(4 * u)
                    steps(4 * u + 1)
                    if not (first and u == 0):
                        product(t if u else t - 1, (u - 1) % UNITS, (p + u - 1) % 2, prod[p] if u else prod[1 - p])
                    steps(4 * u + 2)
                    steps(4 * u + 3)

            periods(pool, period)
            product(NT - 1, UNITS - 1, (1 + UNITS - 1) % 2, prod[1])
            close_sums(*of(NT // 2 - 1, 1))

        @block.scalar
        def _(act):
            act.preload_act_table_set("natural_log_exp_and_others")
            def rbf(t, p, j):
                c = j // 2
                act.wait_ge(arg_done, 9 * t + j + 1)
                upto(act, v1_done, 9 * t + (c - 1 if c < 2 else 2 * c - 2))
                act.activation(ebuf_of(p, c)[:, 512 * (j % 2):512 * (j % 2) + 512], ps_arg[:, :], ACT.Exp).then_inc(e_done, 1)

            def exp1(t, u, q):
                act.wait_ge(v1_done, 9 * t + u + 1)
                act.activation(sbuf1[q][:, :], ps_v1[:, :], ACT.Exp, bias=b1c[:, 0:1]).then_inc(s1_done, 1)

            def log1(t, u, q):
                act.wait_ge(s1_done, 9 * t + u + 1)
                upto(act, v2_done, 9 * t + u - 1)
                act.activation(hbuf[q][:, :], sbuf1[q][:, :], ACT.Ln, bias=1.0).then_inc(h_done, 1)

            def exp2(t, u, q):
                act.wait_ge(v2_done, 9 * t + u + 1)
                upto(act, t2_done, 9 * t + u - 1)
                act.activation(wbuf[q][:, :], ps_v2[:, :], ACT.Exp).then_inc(w_done, 1)

            def log2(T, k, p, i):
                act.wait_ge(prod_done, 9 * T + (4, 6, 9)[i])
                upto(act, sred_done, T - 1)
                upto(act, stail_step, TAIL * (T - 1))
                r = slice(i * QP, i * QP + QP)
                act.activation(lq[p][:, :, r], prod[p][:, :, r], ACT.Ln).then_inc(lq_done, 1)

            def copy_adjT(T, k, p):
                act.wait_ge(adjT_pe, T + 1)
                upto(act, gcn_pe, T)
                act.copy(adj_tr[:, :, :].rearrange("n g m -> n (g m)"), ps_a[:, :]).then_inc(adjT_done, 1)

            def copy_hT(T, j):
                act.wait_ge(hT_pe, 2 * T + j + 1)
                act.copy(hT[:, :, :].rearrange("n g m -> n (g m)"), ps_a[:, 0:256]).then_inc(hT_done, 1)

            def twice_b3(T, k, p):
                act.wait_ge(g3_pe, T + 1)
                act.mul(b3x2[:, :, :].rearrange("n g m -> n (g m)"), ps_a[:, 0:256], 2.0).then_inc(g3_done, 1)

            def twice_b2(T, k, p):
                act.wait_ge(g2_pe, T + 1)
                act.mul(b2x2[:, :, :].rearrange("n g m -> n (g m)"), ps_a[:, 0:256], 2.0).then_inc(g2_done, 1)

            def copy_ranked(T, k, p, j):
                act.wait_ge(pr_pe, 2 * T + j + 1)
                upto(act, rows_out, ROWS_DMA * T)
                upto(act, check_step, CHECKS * T)
                act.copy(parts_r[:, 2 * j:2 * j + 2, :, :].rearrange("r g q s -> r (g q s)"), ps_rank[:, 0:2 * PW]).then_inc(pr_done, 1)

            def copy_permT(T, k, p):
                act.wait_ge(permT_pe, T + 1)
                upto(act, sperm_pe, T - 1)
                act.copy(perm_t[p][:, :, :].rearrange("r g n -> r (g n)"), ps_rank16).then_inc(permT_done, 1)

            def copy_h2T(T, k, p):
                act.wait_ge(h2T_pe, T + 1)
                upto(act, dots_pe, T)
                for e in range(2):
                    m = act.copy(h2T[64 * e:64 * e + 64, e::2, :],
                                 ps_b[64 * e:64 * e + 64, 0:256].rearrange("f (h n) -> f h n", h=2))
                m.then_inc(h2T_done, 1)

            def copy_nT(T, k, p):
                act.wait_ge(nT_pe, T + 1)
                act.copy(nT[:, :], ps_b[0:G, 0:128]).then_inc(nT_done, 1)

            def log_D(T, k, p):
                act.wait_ge(D_pe, T + 1)
                act.activation(lnD[:, :], ps_b[:, :], ACT.Ln, bias=epsc[:, 0:1]).then_inc(lnD_done, 1)

            def recip_D(T, k, p):
                act.wait_ge(lnD_done, T + 1)
                act.activation(rD[:, :], lnD[:, :], ACT.Exp, scale=-1.0).then_inc(rD_done, 1)

            def exp_logits(T, k, p):
                act.wait_ge(lsh_done, T + 1)
                upto(act, pT_pe, T)
                act.activation(pexp[:, :, :], lsh[:, :, :], ACT.Exp).then_inc(pexp_done, 1)

            def copy_pT(T, k, p):
                act.wait_ge(pT_pe, T + 1)
                act.copy(pT[:, :, :].rearrange("n g m -> n (g m)"), ps_b[:, :]).then_inc(pT_done, 1)

            def copy_sR(T, k, p):
                act.wait_ge(sT_pe, T + 1)
                act.copy(sR[:, :, :].rearrange("n g m -> n (g m)"), ps_rank[:, 0:256]).then_inc(sR_done, 1)

            t0 = of(0, 0)
            act.wait_ge(tables_in, 32)
            act.wait_ge(consts_in, N_CONST)
            copy_adjT(*t0)
            act.activation(setup[:, 0:1], c32s[:, C_BIAS:C_BIAS + 1], ACT.Exp).then_inc(setup_act, 1)
            act.wait_ge(setup_dve, 3)
            act.activation(einv[:, :], b2p[:, :], ACT.Exp, scale=-1.0)
            act.activation(setup[:, 1:4], setup[:, 1:4], ACT.Exp).then_inc(setup_act, 1)
            act.wait_ge(setup_act, 2)
            act.activation(setup[:, 4:7], setup[:, 1:4], ACT.Ln, bias=1.0).then_inc(setup_act, 1)
            act.wait_ge(setup_dve, 4)
            act.activation(setup[:, 9:10], setup[:, 8:9], ACT.Exp).then_inc(setup_act, 1)
            act.wait_ge(setup_act, 4)
            act.activation(setup[:, 10:11], setup[:, 9:10], ACT.Ln, bias=1.0).then_inc(setup_act, 1)
            for j in range(2):
                copy_ranked(*t0, j)
            copy_hT(0, 0)
            twice_b3(*t0)
            twice_b2(*t0)
            rbf(0, 0, 0)
            rbf(0, 0, 1)
            copy_permT(*t0)
            copy_hT(0, 1)

            def period(k, p, nxt, nxt2):
                t, k0, p0 = of(k, p)
                n = of(k, p, 1)
                c = of(k, p)
                b = of(k, p, -1)
                first = isinstance(k, int) and k == 0 and p == 0
                def steps(slot):
                    def at(name, f, *a):
                        if ACT_AT[name] == slot:
                            f(*a)

                    if nxt:
                        at("copy_adjT", copy_adjT, *n)
                        at("copy_hT0", copy_hT, n[0], 0)
                        at("copy_ranked0", copy_ranked, *n, 0)
                        at("copy_ranked1", copy_ranked, *n, 1)
                        at("twice_b3", twice_b3, *n)
                        at("twice_b2", twice_b2, *n)
                        at("copy_hT1", copy_hT, n[0], 1)
                    if not first:
                        at("log22", log2, *b, 2)
                        at("copy_sR", copy_sR, *b)
                    if nxt:
                        at("copy_permT", copy_permT, *n)
                    at("copy_h2T", copy_h2T, *c)
                    at("copy_nT", copy_nT, *c)
                    at("log_D", log_D, *c)
                    at("recip_D", recip_D, *c)
                    at("log20", log2, *c, 0)
                    at("exp_logits", exp_logits, *c)
                    at("copy_pT", copy_pT, *c)
                    at("log21", log2, *c, 1)

                for u in range(UNITS):
                    exp1(t, u, (p + u) % 2)
                    steps(4 * u)
                    if u + 2 < UNITS:
                        rbf(t, p, u + 2)
                    elif nxt:
                        rbf(t + 1, 1 - p, u + 2 - UNITS)
                    steps(4 * u + 1)
                    log1(t, u, (p + u) % 2)
                    steps(4 * u + 2)
                    if not (first and u == 0):
                        exp2(t if u else t - 1, (u - 1) % UNITS, (p + u - 1) % 2)
                    steps(4 * u + 3)

            periods(act, period)
            exp2(NT - 1, UNITS - 1, (1 + UNITS - 1) % 2)
            log2(*of(NT // 2 - 1, 1), 2)
            copy_sR(*of(NT // 2 - 1, 1))

            def softplus(act, ps, bias, v):
                act.activation(gabs, ps, ACT.Abs, bias=bias[0:F, 0:1]).then_inc(gabs_done, 1)
                act.activation(grel, ps, ACT.Relu, bias=bias[0:F, 0:1])
                act.wait_ge(gabs_done, v)
                act.activation(gexp, gabs, ACT.Exp, scale=-1.0).then_inc(gexp_done, 1)
                act.wait_ge(gexp_done, v)
                act.activation(glog, gexp, ACT.Ln, bias=1.0).then_inc(gsp_done, 1)

            def body(act):
                def round_(it):
                    for s in range(STEPS):
                        n = STEPS * it + s
                        act.wait_ge(gbc_pe, n + 1)
                        act.activation(gsq[:, 0:W], ps_v1[:, 0:W], ACT.Square, bias=c32s[:, C_CEN:C_CEN + 1])
                        act.activation(gsq[0:KALL - 128, W:2 * W], ps_v1[0:KALL - 128, 0:W], ACT.Square,
                                       bias=c32s[0:KALL - 128, C_CEN + 1:C_CEN + 2]).then_inc(gsq_done, 1)
                        act.wait_ge(gsq_done, n + 1)
                        act.activation(ge[:, 0:W], gsq[:, 0:W], ACT.Exp, scale=-GAMMA)
                        act.activation(ge[0:KALL - 128, W:2 * W], gsq[0:KALL - 128, W:2 * W], ACT.Exp, scale=-GAMMA)\
                            .then_inc(ge_done, 1)
                        act.wait_ge(gv1_pe, n + 1)
                        softplus(act, ps_v2[0:F, 0:W], b1c, 2 * n + 1)
                        act.wait_ge(gv2_pe, n + 1)
                        softplus(act, ps_v2[0:F, W:2 * W], b2p, 2 * n + 2)
                        act.wait_ge(gT_pe, n + 1)
                        if s == 0:
                            upto(act, grow_out, 16 * it)
                        act.copy(grow[:, s, :], ps_a[0:4, 0:F]).then_inc(grow_done, 1)

                loop(act, ROUNDS, round_)

            general(act, body)

        @block.tensor
        def _(pe):
            def arg(t, j, p):
                if j == 0:
                    pe.wait_ge(rows_in, 16 * (t + 1))
                upto(pe, e_done, 9 * t + j)
                pe.matmul(ps_arg[:, :], c16s[:, H_ARGW:H_ARGW + 128],
                          argin[p][:, 512 * j:512 * j + 512], start=True, stop=True).then_inc(arg_done, 1)

            def layer1(t, p, u, i):
                c, h = u // 2, u % 2
                e = ebuf_of(p, c)
                if i == 0:
                    pe.wait_ge(e_done, 9 * t + min(2 * c + 2, UNITS))
                    upto(pe, s1_done, 9 * t + u)
                pair, cols = (h, slice(512 * i, 512 * i + 512)) if u < UNITS - 1 else (i, slice(0, 512))
                m = pe.matmul(ps_v1[:, 512 * i:512 * i + 512], w1z[:, pair, :], e[:, cols], start=True, stop=True)
                if i == 1:
                    m.then_inc(v1_done, 1)

            def layer2(t, u, q, i):
                if i == 0:
                    pe.wait_ge(h_done, 9 * t + u + 1)
                    upto(pe, w_done, 9 * t + u)
                r = slice(512 * i, 512 * i + 512)
                m = pe.matmul(ps_v2[:, r], w2bd[:, :], hbuf[q][:, r], start=True, stop=True)
                if i == 1:
                    m.then_inc(v2_done, 1)

            def adjT(T, k, p):
                pe.wait_ge(adj_in[p], 32 * (k + 1))
                upto(pe, gcn_done, T)
                for g in range(G):
                    m = pe.transpose(ps_a[:, 128 * g:128 * g + 128], adj_t[p][:, g, :], ident)
                m.then_inc(adjT_pe, 1)

            def hT_(T, j):
                pe.wait_ge(lnA["h"], 2 * T + j + 1)
                if j == 0:
                    pe.wait_ge(adjT_done, T + 1)
                else:
                    pe.wait_ge(rsp_done, 2 * T + 2)
                for h in range(2):
                    m = pe.transpose(ps_a[:, 128 * h:128 * h + 128],
                                     hcur[:, 2 * h:2 * h + 2, :].rearrange("n g f -> n (g f)"), ident)
                m.then_inc(hT_pe, 1)

            def feat(h, w, stop):
                return pe.matmul(ps_a[:, 128 * h:128 * h + 128], hT[:, h, :], w, start=True, stop=stop)

            def cheb(T, order, rhs, done, v, signal):
                pe.wait_ge(done, v)
                for h in range(2):
                    m = feat(h, th[:, order, :], rhs is None)
                    if rhs is not None:
                        for g in (2 * h, 2 * h + 1):
                            m = pe.matmul(ps_a[:, F * g:F * g + F], adj_tr[:, g, :], rhs[:, g, :], start=False, stop=g % 2 == 1)
                m.then_inc(signal, 1)

            def row_sums(T, k, p):
                pe.wait_ge(x1_done, T + 1)
                for g in range(G):
                    m = pe.matmul(ps_a[:, g:g + 1], adj_tr[:, g, :], onesc[:, :], start=True, stop=True)
                m.then_inc(rs_done, 1)

            def hw(T, k, p):
                pe.wait_ge(hT_done, 2 * T + 2)
                for h in range(2):
                    m = feat(h, wks[:, :], True)
                m.then_inc(hw_pe, 1)

            def gcn_mm(T, k, p):
                pe.wait_ge(y_done, T + 1)
                pe.matmul(ps_a[:, 0:G * F], ident, ysc[:, :, :].rearrange("n g f -> n (g f)"), start=True, stop=False)
                for g in range(G):
                    m = pe.matmul(ps_a[:, F * g:F * g + F], adj_tr[:, g, :], ysc[:, g, :], start=False, stop=g == G - 1)
                m.then_inc(gcn_pe, 1)

            def delta(T, k, p):
                pe.wait_ge(diag_done, T + 1)
                upto(pe, permT_done, T)
                for g in range(G):
                    o = ps_rank[:, 128 * g:128 * g + 128]
                    pe.matmul(o, id16, c16s[:, H_CMAT:H_CMAT + 128], start=True, stop=False)
                    pe.matmul(o, c16s[:, H_P128:H_P128 + 128], diag[:, g, :], start=False, stop=False)
                    m = pe.matmul(o, diag[:, g, :], c16s[:, H_N128:H_N128 + 128], start=False, stop=True)
                m.then_inc(delta_done, 1)

            def rank_parts(T, k, p, j):
                pe.wait_ge(perm_done, T + 1)
                pe.wait_ge(parts_done, T + 1)
                if j:
                    pe.wait_ge(pr_done, 2 * T + 1)
                for i in range(2):
                    g = 2 * j + i
                    m = pe.matmul(ps_rank[:, PW * i:PW * i + PW], perm[:, g, :], parts[:, g, :, :].rearrange("r q s -> r (q s)"), start=True, stop=True)
                m.then_inc(pr_pe, 1)

            def permT(T, k, p):
                pe.wait_ge(pr_done, 2 * T + 2)
                upto(pe, osum_done, T - 1)
                for g in range(G):
                    m = pe.transpose(ps_rank16[:, 128 * g:128 * g + 128], perm[:, g, :], id16)
                m.then_inc(permT_pe, 1)

            def sT_mm(T, k, p, ranked):
                pe.wait_ge(stail_step, TAIL * (T + 1))
                pe.wait_ge(permT_done, T + 2 if ranked else T + 1)
                if ranked:
                    pe.wait_ge(pr_done, 2 * T + 6)
                for h in range(2):
                    m = pe.transpose(ps_rank[:, 128 * h:128 * h + 128], sT[:, h, :], ident)
                m.then_inc(sT_pe, 1)

            def sperm(T, k, p):
                pe.wait_ge(sR_done, T + 1)
                for g in range(G):
                    m = pe.matmul(ps_rank[:, F * g:F * g + F], perm_t[p][:, g, :], sR[:, g, :], start=True, stop=True)
                m.then_inc(sperm_pe, 1)

            def h2T_mm(T, k, p):
                pe.wait_ge(lnB["h"], 2 * T + 1)
                upto(pe, att_done, T)
                for h in range(2):
                    m = pe.transpose(ps_b[:, 128 * h:128 * h + 128], h2[:, 2 * h:2 * h + 2, :].rearrange("n g f -> n (g f)"), ident)
                m.then_inc(h2T_pe, 1)

            def nT_mm(T, k, p):
                pe.wait_ge(nrm_done, T + 1)
                pe.wait_ge(h2T_done, T + 1)
                pe.transpose(ps_b[0:G, 0:128], nrm[:, :], ident).then_inc(nT_pe, 1)

            def D_mm(T, k, p):
                pe.wait_ge(nTm_done, T + 1)
                pe.matmul(ps_b[:, :], nT[:, :], nTm[:, :, :].rearrange("b g m -> b (g m)"), start=True, stop=True)\
                    .then_inc(D_pe, 1)

            def dots(T, k, p):
                pe.wait_ge(lnD_done, T + 1)
                for g in range(G):
                    m = pe.matmul(ps_b[:, 128 * g:128 * g + 128], h2T[:, g, :], h2T[:, g, :], start=True, stop=True)
                m.then_inc(dots_pe, 1)

            def pT_mm(T, k, p):
                pe.wait_ge(pexp_done, T + 1)
                for g in range(G):
                    m = pe.transpose(ps_b[:, 128 * g:128 * g + 128], pexp[:, g, :], ident)
                m.then_inc(pT_pe, 1)

            def att_mm(T, k, p):
                pe.wait_ge(h2o_done, T + 1)
                pe.wait_ge(pT_done, T + 1)
                for g in range(G):
                    m = pe.matmul(ps_b[:, (F + 1) * g:(F + 1) * (g + 1)], pT[:, g, :], h2o[:, g, :], start=True, stop=True)
                m.then_inc(att_pe, 1)

            t0 = of(0, 0)
            pe.wait_ge(tables_in, 32)
            adjT(*t0)
            delta(*t0)
            pe.wait_ge(consts_in, N_CONST)
            pe.wait_ge(setup_dve, 1)
            pe.wait_ge(setup_act, 1)
            emax = c32s[:, C_EMAX:C_EMAX + 1]
            pe.matmul(ps_v1[:, 0:1], w1z[:, 0, :], setup[:, 0:1], start=True, stop=True)
            pe.matmul(ps_v1[:, 1:2], wpos1[:, :], emax, start=True, stop=True)
            pe.matmul(ps_v1[:, 2:3], wneg1[:, :], emax, start=True, stop=True)
            pe.matmul(ps_v1[:, 3:4], w2bd[:, :], c32s[:, C_NLOG:C_NLOG + 1], start=True, stop=True).then_inc(setup_pe, 1)
            pe.wait_ge(setup_act, 3)
            pe.matmul(ps_v2[:, 0:1], w2bd[:, :], setup[:, 4:5], start=True, stop=True)
            pe.matmul(ps_v2[:, 1:2], wpos2[:, :], setup[:, 5:6], start=True, stop=False)
            pe.matmul(ps_v2[:, 1:2], wneg2[:, :], setup[:, 6:7], start=False, stop=True).then_inc(setup_pe, 1)
            rank_parts(*t0, 0)
            rank_parts(*t0, 1)
            hT_(0, 0)
            cheb(0, 3, None, hT_done, 1, g3_pe)
            cheb(0, 2, b3x2, g3_done, 1, g2_pe)
            cheb(0, 1, b2x2, g2_done, 1, g1_pe)
            pe.wait_ge(setup_dve, 4)
            arg(0, 0, 0)
            cheb(0, 0, d1, g1_done, 1, g0_pe)
            arg(0, 1, 0)
            permT(*t0)
            row_sums(*t0)
            arg(0, 2, 0)
            layer1(0, 0, 0, 0)
            layer1(0, 0, 0, 1)
            hT_(0, 1)
            hw(*t0)
            gcn_mm(*t0)

            def period(k, p, nxt, nxt2):
                t, k0, p0 = of(k, p)
                n = of(k, p, 1)
                c = of(k, p)
                b = of(k, p, -1)
                first = isinstance(k, int) and k == 0 and p == 0
                def steps(slot):
                    def at(name, f, *a):
                        if PE_AT[name] == slot:
                            f(*a)

                    if nxt:
                        T = n[0]
                        at("adjT", adjT, *n)
                        at("delta", delta, *n)
                        at("hT0", hT_, T, 0)
                        at("rank_parts0", rank_parts, *n, 0)
                        at("cheb3", cheb, T, 3, None, hT_done, 2 * T + 1, g3_pe)
                        at("rank_parts1", rank_parts, *n, 1)
                        at("cheb2", cheb, T, 2, b3x2, g3_done, T + 1, g2_pe)
                        at("cheb1", cheb, T, 1, b2x2, g2_done, T + 1, g1_pe)
                        at("cheb0", cheb, T, 0, d1, g1_done, T + 1, g0_pe)
                        at("row_sums", row_sums, *n)
                        at("hT1", hT_, T, 1)
                        at("hw", hw, *n)
                        at("gcn_mm", gcn_mm, *n)
                    if not first:
                        at("sT_mm", sT_mm, *b, nxt)
                        at("sperm", sperm, *b)
                    if nxt:
                        at("permT", permT, *n)
                    at("h2T_mm", h2T_mm, *c)
                    at("nT_mm", nT_mm, *c)
                    at("D_mm", D_mm, *c)
                    at("dots", dots, *c)
                    at("pT_mm", pT_mm, *c)
                    at("att_mm", att_mm, *c)

                for u in range(UNITS):
                    for i in range(2):
                        if u < UNITS - 1:
                            layer1(t, p, u + 1, i)
                        elif nxt:
                            layer1(t + 1, 1 - p, 0, i)
                        if i == 1:
                            if u + 3 < UNITS:
                                arg(t, u + 3, p)
                            elif nxt:
                                arg(t + 1, u + 3 - UNITS, 1 - p)
                        steps(4 * u + i)
                    for i in range(2):
                        layer2(t, u, (p + u) % 2, i)
                        steps(4 * u + 2 + i)

            periods(pe, period)
            sT_mm(*of(NT // 2 - 1, 1), False)
            sperm(*of(NT // 2 - 1, 1))
            pe.wait_ge(osum_done, NT)
            pe.wait_ge(check_step, CHECKS * NT + 1)
            pe.transpose(ps_a[0:1, 0:128], bad[:, :], ident).then_inc(flag_pe, 1)

            def body(pe):
                pe.wait_ge(gw_in, 32)
                pe.wait_ge(gones_done, 1)
                def round_(it):
                    pe.wait_ge(gd_in, 32 * it + 32)
                    for s in range(STEPS):
                        n = STEPS * it + s
                        upto(pe, gsq_done, n)
                        pe.matmul(ps_v1[:, 0:W], gones, gd[s // 2][:, W * (s % 2):W * (s % 2) + W], start=True, stop=True)\
                            .then_inc(gbc_pe, 1)
                        pe.wait_ge(ge_done, n + 1)
                        upto(pe, gsp_done, 2 * n)
                        pe.matmul(ps_v2[0:F, 0:W], gw1[0], ge[:, 0:W], start=True, stop=False)
                        pe.matmul(ps_v2[0:F, 0:W], gw1[1], ge[0:KALL - 128, W:2 * W], start=False, stop=True).then_inc(gv1_pe, 1)
                        pe.wait_ge(gh_done, n + 1)
                        pe.matmul(ps_v2[:, W:2 * W], w2bd[:, :], gh, start=True, stop=True).then_inc(gv2_pe, 1)
                        pe.wait_ge(gsum_done, n + 1)
                        upto(pe, grow_done, n)
                        pe.transpose(ps_a[0:4, 0:128], gsum.rearrange("f a b -> f (a b)"), ident).then_inc(gT_pe, 1)

                loop(pe, ROUNDS, round_)

            general(pe, body)

        @block.vector
        def _(dve):
            def sort_max(T, k, p, r):
                if r == 0:
                    dve.wait_ge(adj_in[p], 32 * (k + 1))
                else:
                    dve.wait_ge(sort_step, SORT_STEPS * T + 2 * r)
                dve.memset(gate[:, :], 0.0)
                for g in range(G):
                    m = dve.max(srt[:, g, 8 * r:8 * r + 8], (srt_w if r else adj_t[p])[:, g, :])
                m.then_inc(sort_step, 1)

            def sort_remove(T, k, p, r):
                dve.wait_ge(sort_step, SORT_STEPS * T + 2 * r + 1)
                dve.memset(gate[:, :], 0.0)
                for g in range(G):
                    m = dve.match_replace(srt_w[:, g, :], srt[:, g, 8 * r:8 * r + 8], (srt_w if r else adj_t[p])[:, g, :], 0.0)
                m.then_inc(sort_step, 1)

            def sort_round(T, k, p, r):
                sort_max(T, k, p, r)
                if r < TOP // 8 - 1:
                    sort_remove(T, k, p, r)

            def counts(T, k, p):
                dve.wait_ge(sort_step, SORT_STEPS * (T + 1))
                upto(dve, diag_done, T)
                dve.tensor_scalar(nz[:, :, :], srt[:, :, :], 0.0, None, ALU.not_equal).then_inc(nz_done, 1)
                dve.tensor_scalar(srt_c[:, :, :], srt[:, :, :], 0.25, -0.25, ALU.min, ALU.max).then_inc(srtc_done, 1)
                dve.wait_ge(nz_done, T + 1)
                dve.tensor_reduce(cnt[:, :], nz[:, :, :], AX.X, ALU.add).then_inc(cnt_done, 1)

            def split_parts(T, k, p):
                def col(q):
                    return parts[:, :, q, 0:TOP]
                upto(dve, pr_pe, 2 * T)
                dve.wait_ge(srtc_done, T + 1)
                dve.tensor_tensor(dsq[:, :, :], srt_c[:, :, :], srt_c[:, :, :], ALU.mult).then_inc(part_step, 1)
                dve.tensor_scalar(col(0), srt_c[:, :, :], DSCALE, None, ALU.mult).then_inc(part_step, 1)
                dve.wait_ge(cnt_done, T + 1)
                dve.tensor_copy(parts[:, :, 0, TOP], cnt[:, :])
                dve.wait_ge(part_step, 3 * T + 2)
                dve.tensor_scalar(col(2), dsq[:, :, :], QSCALE, None, ALU.mult).then_inc(part_step, 1)
                dve.scalar_tensor_tensor(out=col(1), in0=srt_c[:, :, :], scalar=DSCALE, in1=col(0),
                                         op0=ALU.mult, op1=ALU.subtract)
                dve.wait_ge(part_step, 3 * T + 3)
                dve.scalar_tensor_tensor(out=col(3), in0=dsq[:, :, :], scalar=QSCALE, in1=col(2),
                                         op0=ALU.mult, op1=ALU.subtract).then_inc(parts_done, 1)

            def check_sorted(T, k, p):
                upto(dve, check_step, CHECKS * T)
                dve.tensor_scalar(junk4[:, :], srt[:, :, TOP - 1], 1.0, bad[:, 0:1], ALU.mult, ALU.max,
                                  accum_out=bad[:, 0:1]).then_inc(check_step, 1)
                dve.wait_ge(check_step, CHECKS * T + 1)
                dve.tensor_scalar(junk4[:, :], srt[:, :, 0], DMAX, bad[:, 0:1], ALU.subtract, ALU.max,
                                  accum_out=bad[:, 0:1]).then_inc(check_step, 1)

            def check_ranked(T, k, p):
                dve.wait_ge(pr_done, 2 * T + 2)
                dve.wait_ge(check_step, CHECKS * T + 2)
                dve.tensor_scalar(junk4[:, :], parts_r[:, :, 0, TOP], c32s[:, C_CAP:C_CAP + 1], bad[:, 0:1],
                                  ALU.subtract, ALU.max, accum_out=bad[:, 0:1]).then_inc(check_step, 1)

            def negatives(T, k, p):
                dve.wait_ge(adj_in[p], 32 * (k + 1))
                upto(dve, neg_done, T)
                dve.tensor_scalar(junkn[:, :], adj_t[p][:, :, :].rearrange("n g m -> n (g m)"), -1.0, badneg[:, 0:1], ALU.mult,
                                  ALU.max, accum_out=badneg[:, 0:1]).then_inc(neg_done, 1)

            def ranks(T, k, p):
                dve.wait_ge(delta_done, T + 1)
                for g in range(G):
                    m = dve.tensor_scalar(junk[:, g, :], ps_rank[:, 128 * g:128 * g + 128], 0.0, None, ALU.is_gt, ALU.add,
                                          accum_out=rank[:, g:g + 1])
                m.then_inc(rank_done, 1)

            def perms(T, k, p):
                dve.wait_ge(rank_done, T + 1)
                upto(dve, permT_pe, T)
                for g in range(G):
                    m = dve.tensor_scalar(perm[:, g, :], c16s[:, H_IOTA:H_IOTA + 128], rank[:, g:g + 1], None, ALU.is_equal)
                m.then_inc(perm_done, 1)

            def ln_centre(ln, v, src, s, xo):
                dve.tensor_reduce(s[:, :], src[:, :, :], AX.X, ALU.add).then_inc(ln["sum"], 1)
                dve.wait_ge(ln["sum"], v)
                dve.scalar_tensor_tensor(out=xo[:, :, :], in0=bc(s[:, :], F), scalar=-1.0 / F, in1=src[:, :, :],
                                         op0=ALU.mult, op1=ALU.add).then_inc(ln["xc"], 1)

            def ln_var(ln, v, sqr, o):
                dve.wait_ge(ln["sq"], v)
                dve.tensor_reduce(o[:, :], sqr[:, :, :], AX.X, ALU.add).then_inc(ln["var"], 1)
                dve.wait_ge(ln["var"], v)
                dve.tensor_scalar(o[:, :], o[:, :], 1.0 / F, EPS_LN, ALU.mult, ALU.add).then_inc(ln["vareps"], 1)

            def ln_out(ln, v, xo, r, dst):
                dve.wait_ge(ln["rstd"], v)
                dve.scalar_tensor_tensor(out=dst, in0=xo[:, :, :], scalar=0.0, in1=bc(r[:, :], F),
                                         op0=ALU.max, op1=ALU.mult).then_inc(ln["h"], 1)

            def lnA1(T, k, p):
                dve.wait_ge(adj_in[p], 32 * (k + 1))
                ln_centre(lnA, 2 * T + 1, x_t[p], ln_sum, xc)

            def cheb_d1(T, k, p):
                dve.wait_ge(g1_pe, T + 1)
                dve.wait_ge(g3_done, T + 1)
                dve.tensor_tensor(d1[:, :, :].rearrange("n g f -> n (g f)"), ps_a[:, 0:256],
                                  b3x2[:, :, :].rearrange("n g f -> n (g f)"), ALU.subtract).then_inc(g1_done, 1)

            def cheb_x1(T, k, p):
                dve.wait_ge(g0_pe, T + 1)
                dve.tensor_tensor(x1[:, :, :].rearrange("n g f -> n (g f)"), ps_a[:, 0:256],
                                  x_t[p][:, :, :].rearrange("n g f -> n (g f)"), ALU.add).then_inc(x1_done, 1)
                dve.wait_ge(x1_done, T + 1)
                ln_centre(lnA, 2 * T + 2, x1, ln_sum, xc)

            def degrees(T, k, p):
                dve.wait_ge(rs_done, T + 1)
                dve.tensor_scalar(rsp[:, :], ps_a[:, 0:G], 1.0, 1e-30, ALU.add, ALU.max).then_inc(rsp_done, 1)
                dve.tensor_scalar(rsm[:, :], ps_a[:, 0:G], 1.0, 0.0, ALU.add, ALU.is_gt).then_inc(rsp_done, 1)

            def degree_inv(T, k, p):
                dve.wait_ge(dpow_done, T + 1)
                dve.tensor_tensor(dinv[:, :], dinv0[:, :], rsm[:, :], ALU.mult).then_inc(dinv_done, 1)

            def gcn_y(T, k, p):
                dve.wait_ge(hw_pe, T + 1)
                dve.wait_ge(dinv_done, T + 1)
                dve.tensor_tensor(ysc[:, :, :], ps_a[:, 0:256].rearrange("n (g f) -> n g f", g=G), bc(dinv[:, :], F),
                                  ALU.mult).then_inc(y_done, 1)

            def gcn_x2(T, k, p):
                dve.wait_ge(gcn_pe, T + 1)
                dve.scalar_tensor_tensor(out=gcn[:, :, :], in0=ps_a[:, 0:256].rearrange("n (g f) -> n g f", g=G), scalar=0.0,
                                         in1=bc(dinv[:, :], F), op0=ALU.max, op1=ALU.mult).then_inc(gcn_done, 1)
                dve.wait_ge(gcn_done, T + 1)
                dve.tensor_tensor(x2[p][:, :, :], x1[:, :, :], gcn[:, :, :], ALU.add).then_inc(x2_done, 1)

            def lnB1(T, k, p):
                dve.wait_ge(x2_done, T + 1)
                ln_centre(lnB, 2 * T + 1, x2[p], ln2_sum, xc2)

            def norms(T, k, p):
                dve.wait_ge(nsq_done, T + 1)
                dve.tensor_reduce(n2[:, :], sq2[:, :, :], AX.X, ALU.add).then_inc(n2_done, 1)

            def norm_rows(T, k, p):
                dve.wait_ge(nT_done, T + 1)
                dve.tensor_tensor(nTm[:, :, :], nT[:, :].unsqueeze(1).broadcast_to([G, G, 128]),
                                  c32s[0:G, C_NMASK:C_NMASK + 512].rearrange("b (g m) -> b g m", g=G), ALU.mult)\
                    .then_inc(nTm_done, 1)

            def cosines(T, k, p):
                dve.wait_ge(dots_pe, T + 1)
                dve.wait_ge(rD_done, T + 1)
                dve.tensor_tensor(cosm[:, :, :].rearrange("n g m -> n (g m)"), ps_b[:, :], rD[:, :], ALU.mult)\
                    .then_inc(cos_done, 1)

            def logits(T, k, p):
                dve.wait_ge(cos_done, T + 1)
                dve.wait_ge(adj10_done, T + 1)
                dve.scalar_tensor_tensor(out=logit[:, :, :], in0=cosm[:, :, :], scalar=betac[:, 0:1], in1=adj10[p][:, :, :],
                                         op0=ALU.mult, op1=ALU.add).then_inc(logit_done, 1)

            def row_max(T, k, p):
                dve.wait_ge(logit_done, T + 1)
                dve.tensor_reduce(rmax[:, :], logit[:, :, :], AX.X, ALU.max).then_inc(rmax_done, 1)

            def shift(T, k, p):
                dve.wait_ge(rmax_done, T + 1)
                upto(dve, pexp_done, T)
                dve.tensor_tensor(lsh[:, :, :], logit[:, :, :], bc(rmax[:, :], N), ALU.subtract).then_inc(lsh_done, 1)

            def attend(T, k, p):
                o = ps_b[:, 0:G * (F + 1)].rearrange("n (g f) -> n g f", g=G)
                dve.wait_ge(att_pe, T + 1)
                dve.reciprocal(rsum[:, :], o[:, :, F]).then_inc(rsum_done, 1)
                dve.wait_ge(rsum_done, T + 1)
                dve.tensor_tensor(att[:, :, :], o[:, :, 0:F], bc(rsum[:, :], F), ALU.mult).then_inc(att_done, 1)
                dve.wait_ge(att_done, T + 1)
                upto(dve, stash_out, 32 * T)
                dve.tensor_tensor(x3[p][:, :, :], x2[p][:, :, :], att[:, :, :], ALU.add).then_inc(x3_done, 1)
                dve.wait_ge(x3_done, T + 1)
                ln_centre(lnB, 2 * T + 2, x3[p], ln2_sum, xc2)

            def tree(t, u, q, i):
                w = wbuf[q][:, :].rearrange("k (n s) -> k n s", s=4)
                a = t1[q][:, :, :]
                b = t2[q][:, :, :]
                g = UNITS * t + u
                if i == 0:
                    dve.wait_ge(w_done, g + 1)
                    dve.tensor_scalar(a, w[:, :, 2:4], einv[:, 0:1], None, ALU.add).then_inc(t1_done, 1)
                else:
                    dve.wait_ge(t1_done, g + 1)
                    upto(dve, prod_done, g - 1)
                    dve.scalar_tensor_tensor(out=b, in0=w[:, :, 0:2], scalar=einv[:, 0:1], in1=a, op0=ALU.add, op1=ALU.mult)\
                        .then_inc(t2_done, 1)
            def sum_slots(T, k, p):
                dve.wait_ge(lq_done, LQ_PARTS * (T + 1))
                upto(dve, sT_pe, T)
                s0, s, r = BLOCKS[0]
                dve.tensor_reduce(sT[:, :, :], lq[p][:, :, 0:r * s // 4].rearrange("k h (r j) -> k h r j", j=s // 4),
                                  AX.X, ALU.add).then_inc(sred_done, 1)

            def combine(T, k, p):
                dve.wait_ge(sperm_pe, T + 1)
                dve.tensor_tensor(osum[:, :, :].rearrange("n g f -> n (g f)"), ps_rank[:, 0:256],
                                  h4[p][:, :, :].rearrange("n g f -> n (g f)"), ALU.mult).then_inc(osum_done, 1)
                dve.wait_ge(osum_done, T + 1)
                upto(dve, out_out[p], 16 * k)
                dve.tensor_tensor(ofin[p][:, :, :], osum[:, :, :], x3[p][:, :, :], ALU.add).then_inc(ofin_done, 1)

            t0 = of(0, 0)
            for r in range(TOP // 8):
                sort_round(*t0, r)
            counts(*t0)
            lnA1(*t0)
            dve.wait_ge(wz_done, 6)
            split_parts(*t0)
            dve.wait_ge(tables_in, 32)
            dve.wait_ge(consts_in, N_CONST)
            dve.memset(epsc[:, :], EPS_COS)
            dve.tensor_scalar(wpos1[:, :], w1z[:, 0, :], 0.0, None, ALU.max)
            dve.tensor_scalar(wneg1[:, :], w1z[:, 0, :], 0.0, None, ALU.min)
            dve.tensor_scalar(wpos2[:, :], w2bd[:, :], 0.0, None, ALU.max)
            dve.tensor_scalar(wneg2[:, :], w2bd[:, :], 0.0, None, ALU.min)
            for e in range(2):
                r = slice(F * e, F * e + F)
                dve.tensor_copy(th[r, 2:4, r], thin[r, 2:4, :])
                m = dve.tensor_tensor(th[r, 0:2, r], thin[r, 0:2, :], thin[r, 2:4, :], ALU.subtract)
            m.then_inc(setup_dve, 1)
            ln_var(lnA, 1, sq, var)
            ranks(*t0)
            perms(*t0)
            ln_out(lnA, 1, xc, rstd, hcur[:, :, :])
            dve.wait_ge(setup_pe, 1)
            dve.tensor_scalar(b2p[:, :], ps_v1[:, 3:4], b2c[:, 0:1], None, ALU.add).then_inc(setup_dve, 1)
            dve.tensor_scalar(setup[:, 7:8], ps_v1[:, 1:2], b1c[:, 0:1], 40.0, ALU.add, ALU.subtract)
            dve.tensor_scalar(setup[:, 1:4], ps_v1[:, 0:3], b1c[:, 0:1], 60.0, ALU.add, ALU.min).then_inc(setup_dve, 1)
            dve.wait_ge(setup_pe, 2)
            dve.wait_ge(setup_dve, 3)
            dve.tensor_scalar(setup[:, 11:12], ps_v2[:, 1:2], b2p[:, 0:1], 10.0, ALU.add, ALU.subtract)
            dve.tensor_scalar(setup[:, 8:9], ps_v2[:, 0:1], b2p[:, 0:1], 60.0, ALU.add, ALU.min).then_inc(setup_dve, 1)
            dve.tensor_scalar(setup[:, 12:13], b2p[:, :], -1.0, 10.0, ALU.mult, ALU.subtract)
            dve.tensor_scalar(setup[:, 14:15], b2p[:, :], LOG2, float(N), ALU.subtract, ALU.mult).then_inc(setup_dve, 1)
            dve.wait_ge(setup_dve, 5)
            dve.scalar_tensor_tensor(out=bad[:, :], in0=setup[:, 7:8], scalar=setup[:, 12:13], in1=setup[:, 11:12],
                                     op0=ALU.max, op1=ALU.max)
            dve.wait_ge(setup_act, 5)
            dve.tensor_tensor(setup[:, 13:14], setup[:, 10:11], b2p[:, :], ALU.subtract).then_inc(setup_dve, 1)
            dve.wait_ge(setup_dve, 6)
            for h in range(2):
                m = dve.tensor_scalar(kmat[:, h, :], c32s[:, C_MISS:C_MISS + 128], setup[:, 13:14], setup[:, 14:15],
                                      ALU.mult, ALU.add)
            m.then_inc(setup_dve, 1)
            dve.wait_ge(setup_dve, 7)
            check_sorted(*t0)
            negatives(*t0)
            check_ranked(*t0)
            for r in range(4):
                sort_round(*of(0, 1), r)
            cheb_d1(*t0)
            cheb_x1(*t0)
            sort_round(*of(0, 1), 4)
            degrees(*t0)
            ln_var(lnA, 2, sq, var)
            sort_round(*of(0, 1), 5)
            degree_inv(*t0)
            ln_out(lnA, 2, xc, rstd, hcur[:, :, :])
            gcn_y(*t0)
            sort_round(*of(0, 1), 6)
            gcn_x2(*t0)

            def period(k, p, nxt, nxt2):
                t, k0, p0 = of(k, p)
                n = of(k, p, 1)
                m = of(k, p, 2)
                c = of(k, p)
                b = of(k, p, -1)
                first = isinstance(k, int) and k == 0 and p == 0
                def steps(slot):
                    def at(name, f, *a):
                        if DVE_AT[name] == slot:
                            f(*a)

                    if nxt:
                        at("counts", counts, *n)
                        at("negatives", negatives, *n)
                        at("lnA1", lnA1, *n)
                        at("split_parts", split_parts, *n)
                        at("check_sorted", check_sorted, *n)
                        at("ln_var_A1", ln_var, lnA, 2 * t + 3, sq, var)
                        at("ranks", ranks, *n)
                        at("perms", perms, *n)
                        at("ln_out_A1", ln_out, lnA, 2 * t + 3, xc, rstd, hcur[:, :, :])
                        at("check_ranked", check_ranked, *n)
                        at("cheb_d1", cheb_d1, *n)
                        at("cheb_x1", cheb_x1, *n)
                        at("degrees", degrees, *n)
                        at("ln_var_A2", ln_var, lnA, 2 * t + 4, sq, var)
                        at("degree_inv", degree_inv, *n)
                        at("ln_out_A2", ln_out, lnA, 2 * t + 4, xc, rstd, hcur[:, :, :])
                        at("gcn_y", gcn_y, *n)
                        at("gcn_x2", gcn_x2, *n)
                    if nxt2:
                        for r in range(TOP // 8):
                            at(f"max{r}", sort_max, *m, r)
                            if r < TOP // 8 - 1:
                                at(f"remove{r}", sort_remove, *m, r)
                    if not first:
                        at("sum_slots", sum_slots, *b)
                        at("combine", combine, *b)
                    at("lnB1", lnB1, *c)
                    at("ln_var_B1", ln_var, lnB, 2 * t + 1, sq2, var2)
                    at("ln_out_B1", ln_out, lnB, 2 * t + 1, xc2, rstd2, h2[:, :, :])
                    at("norms", norms, *c)
                    at("norm_rows", norm_rows, *c)
                    at("cosines", cosines, *c)
                    at("logits", logits, *c)
                    at("row_max", row_max, *c)
                    at("shift", shift, *c)
                    at("attend", attend, *c)
                    at("ln_var_B2", ln_var, lnB, 2 * t + 2, sq2, var2)
                    at("ln_out_B2", ln_out, lnB, 2 * t + 2, xc2, rstd2, h4[p][:, :, :])

                for u in range(UNITS):
                    tu = (t if u else t - 1, (u - 1) % UNITS, (p + u - 1) % 2)
                    steps(4 * u)
                    steps(4 * u + 1)
                    if not (first and u == 0):
                        tree(*tu, 0)
                    steps(4 * u + 2)
                    if not (first and u == 0):
                        tree(*tu, 1)
                    steps(4 * u + 3)

            periods(dve, period)
            for i in range(2):
                tree(NT - 1, UNITS - 1, (1 + UNITS - 1) % 2, i)
            sum_slots(*of(NT // 2 - 1, 1))
            combine(*of(NT // 2 - 1, 1))
            dve.wait_ge(neg_done, NT)
            dve.wait_ge(check_step, CHECKS * NT)
            dve.tensor_tensor(bad[:, :], bad[:, :], badneg[:, :], ALU.max).then_inc(check_step, 1)
            dve.wait_ge(flag_pe, 1)
            dve.tensor_reduce(flagf[:, :], ps_a[0:1, 0:128], AX.X, ALU.max).then_inc(flag_dve, 1)
            dve.wait_ge(flag_dve, 1)
            dve.tensor_scalar(flagi[:, :], flagf[:, :], 0.0, None, ALU.is_gt).then_inc(flag_dve, 1)

            def body(dve):
                dve.memset(gones, 1.0)
                dve.memset(gh[F:128, :], 0.0)
                dve.memset(gsum[F:128, :, :], 0.0).then_inc(gones_done, 1)
                def round_(it):
                    for s in range(STEPS):
                        n = STEPS * it + s
                        dve.wait_ge(gsp_done, 2 * n + 1)
                        dve.tensor_tensor(gh[0:F, :], grel, glog, ALU.add).then_inc(gh_done, 1)
                        dve.wait_ge(gsp_done, 2 * n + 2)
                        dve.tensor_tensor(gw, grel, glog, ALU.add).then_inc(gw_done, 1)
                        dve.wait_ge(gw_done, n + 1)
                        dve.tensor_reduce(gsum[0:F, :, :].rearrange("f a b -> f (a b)"), gw.rearrange("f (i j) -> f i j", j=N), AX.X, ALU.add)\
                            .then_inc(gred_done, 1)
                        dve.wait_ge(gred_done, n + 1)
                        dve.tensor_scalar(gsum[0:F, :, :], gsum[0:F, :, :], -N * LOG2, None, ALU.add).then_inc(gsum_done, 1)

                loop(dve, ROUNDS, round_)
                def finish(T):
                    dve.wait_ge(gx_in, 48 * T + 48)
                    dve.tensor_tensor(gS[:, :, :], gS[:, :, :], gx[1][:, :, :], ALU.mult).then_inc(gmul_done, 1)
                    dve.wait_ge(gmul_done, T + 1)
                    upto(dve, gout_out, 16 * T)
                    dve.tensor_tensor(ofin[0][:, :, :], gS[:, :, :], gx[0][:, :, :], ALU.add).then_inc(gfin_done, 1)

                loop(dve, NT, finish)

            general(dve, body)


_INS = ["x", "adj", "L0_gnn_theta", "L1_gnn_kernel", "L2_gnn_beta", "L3_gnn_W1", "L3_gnn_b1", "L3_gnn_W2", "L3_gnn_b2"]


def kernel(**inputs):
    import numpy as _np
    import concourse.bacc as _bacc
    from concourse import mybir as _mybir
    from concourse.bass_utils import run_bass_kernel_spmd as _run

    nc = _bacc.Bacc("TRN2", target_bir_lowering=False, num_devices=1)
    arrays, args = {}, []
    c32, c16 = tables()
    for name, a in [(n, _np.ascontiguousarray(inputs[n])) for n in _INS] + [("table32", c32), ("table16", c16)]:
        arrays[f"in_{name}"] = a
        args.append(nc.dram_tensor(f"in_{name}", a.shape, _mybir.dt.from_np(a.dtype), kind="ExternalInput").ap())
    out = nc.dram_tensor("out_0", inputs["x"].shape, _mybir.dt.float32, kind="ExternalOutput").ap()
    adjacency_layers(nc, *args, out)
    return _run(nc, [arrays], core_ids=[0]).results[0]["out_0"]
```
